# Optimizing a Trainium2 kernel written in Bass

```python
import numpy as np
import jax
import jax.numpy as jnp

def _softmax(x, axis=-1):
    return jax.nn.softmax(x, axis=axis)

def _gelu(x):
    return jax.nn.gelu(x, approximate=True)

def _silu(x):
    return jax.nn.silu(x)

def _sigmoid(x):
    return jax.nn.sigmoid(x)

def _layernorm(x, axis=-1, eps=1e-05):
    m = jnp.mean(x, axis=axis, keepdims=True)
    v = jnp.var(x, axis=axis, keepdims=True)
    return (x - m) / jnp.sqrt(v + eps)

def _scatter_add(tgt, idx, src, axis=0):
    return tgt.at[idx].add(src)

def _segment_sum(src, seg, n):
    return jax.ops.segment_sum(src, seg, n)
kernel_name = 'mk_gnn_resnorm_d2_gnn_r32_a7576c'

def setup_inputs(seed: int=0):
    np.random.seed(seed)
    _w = jnp.asarray

    def _rec_inputs():
        import jax
        import jax.numpy as jnp
        _gk = jax.random.key(seed)
        x = -0.0001006 + 1 * jax.random.normal(jax.random.fold_in(_gk, 1), (50000, 96), jnp.float32)
        src = jax.random.randint(jax.random.fold_in(_gk, 2), (25000,), 0, 50000, jnp.int32)
        dst = jax.random.randint(jax.random.fold_in(_gk, 3), (25000,), 0, 50000, jnp.int32)
        _o = jnp.argsort(dst, stable=True)
        src = src[_o]
        dst = dst[_o]
        edge_attr_32 = 0.000196303 + 1.00016 * jax.random.normal(jax.random.fold_in(_gk, 11), (25000, 32), jnp.float32)
        edge_attr_96 = 5.93493e-05 + 1.00006 * jax.random.normal(jax.random.fold_in(_gk, 12), (25000, 96), jnp.float32)
        return (x, src, dst, edge_attr_32, edge_attr_96)
    x, src, dst, edge_attr_32, edge_attr_96 = _rec_inputs()

    def _L0_gnn_setup():
        import jax, jax.numpy as jnp
        import numpy as np
        N, E = (50000, 25000)
        ND, ED = (96, 32)

        def _gelu(x):
            return jax.nn.gelu(x, approximate=False)
        key = jax.random.key(seed)
        ks = jax.random.split(key, 16)
        s = lambda fan_in: 1.0 / np.sqrt(fan_in)
        inp = {'x': jax.random.normal(ks[0], (N, ND), jnp.float32), 'edge_index': jax.random.randint(ks[1], (2, E), 0, N, jnp.int32), 'edge_attr': jax.random.normal(ks[2], (E, ED), jnp.float32), 'mW1': jax.random.uniform(ks[3], (ND + ED, ND), jnp.float32, -s(ND + ED), s(ND + ED)), 'mb1': jnp.zeros((ND,), jnp.float32), 'mW2': jax.random.uniform(ks[4], (ND, ND), jnp.float32, -s(ND), s(ND)), 'mb2': jnp.zeros((ND,), jnp.float32), 'gW1': jax.random.uniform(ks[5], (ND + ED, ND), jnp.float32, -s(ND + ED), s(ND + ED)), 'gb1': jnp.zeros((ND,), jnp.float32), 'gW2': jax.random.uniform(ks[6], (ND, 1), jnp.float32, -s(ND), s(ND)), 'gb2': jnp.zeros((1,), jnp.float32), 'uW1': jax.random.uniform(ks[7], (2 * ND, ND), jnp.float32, -s(2 * ND), s(2 * ND)), 'ub1': jnp.zeros((ND,), jnp.float32), 'uW2': jax.random.uniform(ks[8], (ND, ND), jnp.float32, -s(ND), s(ND)), 'ub2': jnp.zeros((ND,), jnp.float32), 'ln_g': jnp.ones((ND,), jnp.float32), 'ln_b': jnp.zeros((ND,), jnp.float32)}
        return inp
    _L0_gnn_all = _L0_gnn_setup()
    _L0_gnn_in = {k: v for k, v in _L0_gnn_all.items() if k in ('mW1', 'mb1', 'mW2', 'mb2', 'gW1', 'gb1', 'gW2', 'gb2', 'uW1', 'ub1', 'uW2', 'ub2', 'ln_g', 'ln_b')}
    del _L0_gnn_all

    def _L1_gnn_setup():
        import jax, jax.numpy as jnp
        import numpy as np
        N_NODES = 50000
        N_EDGES = 25000
        IN_DIM = 96
        NUM_HEADS = 8
        HEAD_DIM = IN_DIM // NUM_HEADS
        key = jax.random.key(seed)
        ks = jax.random.split(key, 11)
        s = 1.0 / np.sqrt(IN_DIM)
        return {'x': jax.random.normal(ks[0], (N_NODES, IN_DIM), dtype=jnp.float32), 'edge_index': jax.random.randint(ks[1], (2, N_EDGES), 0, N_NODES, dtype=jnp.int64), 'edge_attr': jax.random.normal(ks[2], (N_EDGES, IN_DIM), dtype=jnp.float32), 'Wq': jax.random.normal(ks[3], (IN_DIM, IN_DIM), dtype=jnp.float32) * s, 'bq': jax.random.normal(ks[4], (IN_DIM,), dtype=jnp.float32) * s, 'Wk': jax.random.normal(ks[5], (IN_DIM, IN_DIM), dtype=jnp.float32) * s, 'bk': jax.random.normal(ks[6], (IN_DIM,), dtype=jnp.float32) * s, 'We': jax.random.normal(ks[7], (IN_DIM, IN_DIM), dtype=jnp.float32) * s, 'be': jax.random.normal(ks[8], (IN_DIM,), dtype=jnp.float32) * s, 'Wv': jax.random.normal(ks[9], (IN_DIM, IN_DIM), dtype=jnp.float32) * s, 'bv': jax.random.normal(ks[10], (IN_DIM,), dtype=jnp.float32) * s}
    _L1_gnn_all = _L1_gnn_setup()
    _L1_gnn_in = {k: v for k, v in _L1_gnn_all.items() if k in ('Wq', 'bq', 'Wk', 'bk', 'We', 'be', 'Wv', 'bv')}
    del _L1_gnn_all
    return {'x': x, 'src': src, 'dst': dst, 'edge_attr_32': edge_attr_32, 'edge_attr_96': edge_attr_96, 'L0_gnn_mW1': _L0_gnn_in['mW1'], 'L0_gnn_mb1': _L0_gnn_in['mb1'], 'L0_gnn_mW2': _L0_gnn_in['mW2'], 'L0_gnn_mb2': _L0_gnn_in['mb2'], 'L0_gnn_gW1': _L0_gnn_in['gW1'], 'L0_gnn_gb1': _L0_gnn_in['gb1'], 'L0_gnn_gW2': _L0_gnn_in['gW2'], 'L0_gnn_gb2': _L0_gnn_in['gb2'], 'L0_gnn_uW1': _L0_gnn_in['uW1'], 'L0_gnn_ub1': _L0_gnn_in['ub1'], 'L0_gnn_uW2': _L0_gnn_in['uW2'], 'L0_gnn_ub2': _L0_gnn_in['ub2'], 'L0_gnn_ln_g': _L0_gnn_in['ln_g'], 'L0_gnn_ln_b': _L0_gnn_in['ln_b'], 'L1_gnn_Wq': _L1_gnn_in['Wq'], 'L1_gnn_bq': _L1_gnn_in['bq'], 'L1_gnn_Wk': _L1_gnn_in['Wk'], 'L1_gnn_bk': _L1_gnn_in['bk'], 'L1_gnn_We': _L1_gnn_in['We'], 'L1_gnn_be': _L1_gnn_in['be'], 'L1_gnn_Wv': _L1_gnn_in['Wv'], 'L1_gnn_bv': _L1_gnn_in['bv']}

def reference(x, src, dst, edge_attr_32, edge_attr_96, L0_gnn_mW1, L0_gnn_mb1, L0_gnn_mW2, L0_gnn_mb2, L0_gnn_gW1, L0_gnn_gb1, L0_gnn_gW2, L0_gnn_gb2, L0_gnn_uW1, L0_gnn_ub1, L0_gnn_uW2, L0_gnn_ub2, L0_gnn_ln_g, L0_gnn_ln_b, L1_gnn_Wq, L1_gnn_bq, L1_gnn_Wk, L1_gnn_bk, L1_gnn_We, L1_gnn_be, L1_gnn_Wv, L1_gnn_bv):
    import jax
    import jax.numpy as jnp

    def _L0_gnn_ref(x, edge_index, edge_attr, mW1, mb1, mW2, mb2, gW1, gb1, gW2, gb2, uW1, ub1, uW2, ub2, ln_g, ln_b):
        import jax, jax.numpy as jnp
        import numpy as np
        N, E = (50000, 25000)
        ND, ED = (96, 32)

        def _gelu(x):
            return jax.nn.gelu(x, approximate=False)
        src, dst = (edge_index[0], edge_index[1])
        edge_input = jnp.concatenate([x[src], edge_attr], axis=-1)
        messages = _gelu(edge_input @ mW1 + mb1) @ mW2 + mb2
        gates = jax.nn.sigmoid(_gelu(edge_input @ gW1 + gb1) @ gW2 + gb2)
        aggregated = jax.ops.segment_sum(messages * gates, dst, num_segments=x.shape[0])
        combined = jnp.concatenate([x, aggregated], axis=-1)
        update = _gelu(combined @ uW1 + ub1) @ uW2 + ub2
        h = x + update
        mu = jnp.mean(h, axis=-1, keepdims=True)
        var = jnp.mean(jnp.square(h - mu), axis=-1, keepdims=True)
        return (h - mu) * jax.lax.rsqrt(var + 1e-05) * ln_g + ln_b

    def _L1_gnn_ref(x, edge_index, edge_attr, Wq, bq, Wk, bk, We, be, Wv, bv):
        import jax, jax.numpy as jnp
        import numpy as np
        N_NODES = 50000
        N_EDGES = 25000
        IN_DIM = 96
        NUM_HEADS = 8
        HEAD_DIM = IN_DIM // NUM_HEADS
        N = x.shape[0]
        H, D = (NUM_HEADS, HEAD_DIM)
        Q_h = (x @ Wq + bq).reshape(N, H, D)
        K_h = (x @ Wk + bk).reshape(N, H, D)
        V_h = (x @ Wv + bv).reshape(N, H, D)
        E = (edge_attr @ We + be).reshape(-1, H, D)
        src_idx = edge_index[0]
        dst_idx = edge_index[1]
        src = K_h[src_idx]
        dest = Q_h[dst_idx]
        score = src * dest / jnp.sqrt(jnp.asarray(D, x.dtype))
        score = score * E
        score = jnp.exp(jnp.clip(score.sum(-1, keepdims=True), -5.0, 5.0))
        msg = V_h[src_idx] * score
        wV = jax.ops.segment_sum(msg, dst_idx, num_segments=N)
        Z = jax.ops.segment_sum(score, dst_idx, num_segments=N)
        h_out = wV / (Z + 1e-06)
        return h_out.reshape(N, H * D)
    edge_index = jnp.stack([src, dst])
    x = _layernorm(x + _L0_gnn_ref(x, edge_index, edge_attr_32, L0_gnn_mW1, L0_gnn_mb1, L0_gnn_mW2, L0_gnn_mb2, L0_gnn_gW1, L0_gnn_gb1, L0_gnn_gW2, L0_gnn_gb2, L0_gnn_uW1, L0_gnn_ub1, L0_gnn_uW2, L0_gnn_ub2, L0_gnn_ln_g, L0_gnn_ln_b), axis=-1)
    x = _layernorm(x + _L1_gnn_ref(x, edge_index, edge_attr_96, L1_gnn_Wq, L1_gnn_bq, L1_gnn_Wk, L1_gnn_bk, L1_gnn_We, L1_gnn_be, L1_gnn_Wv, L1_gnn_bv), axis=-1)
    return x

_drawn_inputs = setup_inputs


def setup_inputs(seed=0):
    import zlib

    import numpy as np

    out = dict(_drawn_inputs(seed))
    spreads = {'L0_gnn_mb1': (0.0, 2.0),
     'L0_gnn_mb2': (0.0, 2.0),
     'L0_gnn_gb1': (0.0, 2.0),
     'L0_gnn_ub1': (0.0, 0.439),
     'L0_gnn_ub2': (0.0, 0.1),
     'L0_gnn_ln_g': (1.0, 0.2),
     'L0_gnn_ln_b': (0.0, 0.1)}
    factors = {'edge_attr_32': 8.0,
     'L0_gnn_mW1': 8.0,
     'L0_gnn_mW2': 8.0,
     'L0_gnn_gW1': 8.0,
     'L0_gnn_gW2': 8.0,
     'L1_gnn_bq': 6.228,
     'L1_gnn_bk': 6.401,
     'L1_gnn_be': 5.57}
    for name, (base, spread) in spreads.items():
        noise = np.random.default_rng([zlib.crc32(name.encode()), seed]).standard_normal(out[name].shape)
        drawn = base * np.exp(spread * noise) if base else spread * noise
        out[name] = jnp.asarray(drawn.astype(out[name].dtype))
    for name, factor in factors.items():
        out[name] = (out[name] * factor).astype(out[name].dtype)
    return out
```

```python
from contextlib import ExitStack

import numpy as np

import concourse.bass as bass
from concourse import mybir

P = 128
N, E, D, DE = 50000, 25000, 96, 32
HEADS = 8
HD = D // HEADS
DH = D + HEADS
EJ = 4
EROWS = P * EJ
EGROUPS = -(-E // EROWS)
EFULL = EGROUPS - 1
ETAIL_P = (E - EFULL * EROWS) // EJ
NJ = 8
NROWS = P * NJ
NGROUPS = -(-N // NROWS)
FAR = 1 << 20
BANK = 512
MAGIC = 0x5F3759DF
EPS = 1e-5

F32 = mybir.dt.float32
I32 = mybir.dt.int32
ALU = mybir.AluOpType
ACT = mybir.ActivationFunctionType

assert E % EJ == 0 and EGROUPS == NGROUPS


def sweep(eng, start, stop, front, back, step):
    first, last = start + front, stop - back
    last -= (last - first) % 2
    for i in range(start, first):
        step(i, i % 2, False)
    with eng.Fori(first, last - 1, 2) as i:
        step(i, first % 2, True)
        step(i + 1, (first + 1) % 2, True)
    for i in range(last, stop):
        step(i, i % 2, False)


def per_slot(i, slot):
    return i * 8 + (16 - 8 * slot)


def build(nc, x, src, dst, ea32, ea96, mW1, mb1, mW2, mb2, gW1, gb1, gW2, gb2, uW1, ub1, uW2, ub2,
          ln_g, ln_b, Wq, bq, Wk, bk, We, be, Wv, bv, ident_c, heads_c, spare_c, out):
    with ExitStack() as ctx:
        def sb(name, shape, dt=F32):
            return ctx.enter_context(nc.sbuf_tensor(name, shape, dt))

        def sem(name):
            return ctx.enter_context(nc.semaphore(name))

        pre_d = nc.dram_tensor("pre_d", [N + EROWS, D], F32).ap()
        x1_d = nc.dram_tensor("x1_d", [N, D], F32).ap()
        cont_d = nc.dram_tensor("cont_d", [1, EGROUPS * EROWS + EJ], F32).ap()

        ident = sb("ident", [P, P])
        heads = sb("heads", [D, DH])
        mW1s, gW1s = sb("mW1s", [P, D]), sb("gW1s", [P, D])
        mW2s, gW2c, gW2s = sb("mW2s", [D, D]), sb("gW2c", [D, 1]), sb("gW2s", [D, D])
        uW1x, uW1a, uW2s = sb("uW1x", [D, D]), sb("uW1a", [D, D]), sb("uW2s", [D + 1, D])
        Wqs, Wks, Wes, Wvs = sb("Wqs", [D, D]), sb("Wks", [D, D]), sb("Wes", [D, D]), sb("Wvs", [D, DH])
        mb1s, gb1s, mb2s, gb2s, ub1s = (sb(n, [D, 1]) for n in ("mb1s", "gb1s", "mb2s", "gb2s", "ub1s"))
        bqs, bks, bes, bvs = sb("bqs", [D, 1]), sb("bks", [D, 1]), sb("bes", [D, 1]), sb("bvs", [DH, 1])
        lng, lnb = sb("lng", [P, D]), sb("lnb", [P, D])
        zeros = sb("zeros", [P, EJ * D])
        src_i, dst_i, next_i = (sb(n, [P, EGROUPS, EJ], I32) for n in ("src_i", "dst_i", "next_i"))
        spare = sb("spare", [P, EJ], I32)
        same = sb("same", [P, EGROUPS, EJ])
        shift = sb("shift", [P, EGROUPS, EJ])
        add_at = sb("add_at", [P, EGROUPS, EJ], I32)
        put_at = sb("put_at", [P, EGROUPS, EJ], I32)
        dst_at = sb("dst_at", [P, EGROUPS, EJ], I32)
        rows = sb("rows", [P, EGROUPS * EJ, D])

        x_in = sb("x_in", [P, 2, NJ * D])
        pre_io = sb("pre_io", [P, 2, NJ * D])
        nT = sb("nT", [D + 1, 2, NJ * P])
        h, xb, y = (sb(n, [P, 2, NJ * D]) for n in ("h", "xb", "y"))
        x1o, oo = sb("x1o", [P, 2, NJ * D]), sb("oo", [P, 2, NJ * D])
        bn = sb("bn", [P, 2, NJ, 6])
        msum, mdif, sqs, nv = (sb(n, [P, k, NJ]) for n, k in (("msum", 2), ("mdif", 2), ("sqs", 2), ("nv", 3)))
        nvar, nroot, nhalf = sb("nvar", [P, 3, NJ]), sb("nroot", [P, 3, NJ]), sb("nhalf", [P, 3, NJ])
        nscale, nshift = sb("nscale", [P, 2, 3, NJ]), sb("nshift", [P, 2, 2, NJ])

        ein = sb("ein", [P, 2, EJ, D + DE])
        einT = sb("einT", [P, 2, EROWS])
        gm, gg, gate, mm = (sb(n, [D, EROWS]) for n in ("gm", "gg", "gate", "mm"))
        mask = sb("mask", [DH, 2, EROWS])
        seg = sb("seg", [DH, 2, EROWS])

        x1s = sb("x1s", [P, 2, EJ, D])
        x1d = sb("x1d", [P, 2, EJ, D])
        ea = sb("ea", [P, 2, EJ, D])
        kS, kq, kqe = (sb(n, [D, EROWS]) for n in ("kS", "kq", "kqe"))
        clip, score, msg = (sb(n, [DH, EROWS]) for n in ("clip", "score", "msg"))
        yc, fin = sb("yc", [P, 2, EJ, D]), sb("fin", [P, 2, EJ, D])
        hc = sb("hc", [P, EJ, D])
        zr = sb("zr", [P, 2, EJ, HEADS])
        cbn = sb("cbn", [P, EJ, 6])
        csum, cdif, csqs, cv = (sb(n, [P, EJ]) for n in ("csum", "cdif", "csqs", "cv"))
        cvar, croot, chalf = sb("cvar", [P, EJ]), sb("croot", [P, EJ]), sb("chalf", [P, EJ])
        cscale, cshift = sb("cscale", [P, 2, EJ]), sb("cshift", [P, 2, EJ])

        ps = ctx.enter_context(nc.psum_tensor("ps", [P, 8, BANK], F32))

        def two_banks(b):
            return ps[:, b:b + 2, 0:EJ * D]

        nTf = nT[0:D, :, :].rearrange("p s c -> p (s c)")
        opT = [[nTf[:, 0:512], nTf[:, 512:1024], nTf[:, 1024:1536]],
               [nTf[:, 1536:2048], einT[0:D, 0, :], einT[0:D, 1, :]]]

        pads_set = sem("pads_set")
        weights_loaded, index_loaded = sem("weights_loaded"), sem("index_loaded")
        index_made, same_made, cont_stored = sem("index_made"), sem("same_made"), sem("cont_stored")
        weights_made, spare_zeroed = sem("weights_made"), sem("spare_zeroed")
        x_loaded = [sem("x_loaded0"), sem("x_loaded1")]
        x_turned, xT_copied = sem("x_turned"), sem("xT_copied")
        pre_summed, pre_copied = sem("pre_summed"), sem("pre_copied")
        pre_stored = [sem("pre_stored0"), sem("pre_stored1")]
        xs_gathered = [sem(f"xs_gathered{j}") for j in range(EJ)]
        ein_loaded = [sem("ein_loaded0"), sem("ein_loaded1")]
        ein_turned, einT_copied = sem("ein_turned"), sem("einT_copied")
        hidden_summed, gelu_done = sem("hidden_summed"), sem("gelu_done")
        message_summed, gate_summed = sem("message_summed"), sem("gate_summed")
        tanh_done, gate_done, gated = sem("tanh_done"), sem("gate_done"), sem("gated")
        mask_loaded = [sem("mask_loaded0"), sem("mask_loaded1")]
        scanned, agg_summed, agg_copied = sem("scanned"), sem("agg_summed"), sem("agg_copied")
        agg_added = [sem(f"agg_added{j}") for j in range(EJ)]
        pre_loaded = [sem("pre_loaded0"), sem("pre_loaded1")]
        xn_loaded = [sem("xn_loaded0"), sem("xn_loaded1")]
        pre_turned, node_gelu, update_summed = sem("pre_turned"), sem("node_gelu"), sem("update_summed")
        h_made, xb_made, zg_made, y_made = sem("h_made"), sem("xb_made"), sem("zg_made"), sem("y_made")
        stats_step, root_step, norms_ready = sem("stats_step"), sem("root_step"), sem("norms_ready")
        h_measured, y_measured = sem("h_measured"), sem("y_measured")
        z_made, x1_made, out_made = sem("z_made"), sem("x1_made"), sem("out_made")
        x1_stored = [sem("x1_stored0"), sem("x1_stored1")]
        out_stored = [sem("out_stored0"), sem("out_stored1")]
        xd_gathered = [sem(f"xd_gathered{j}") for j in range(EJ)]
        x1s_gathered = [sem(f"x1s_gathered{j}") for j in range(EJ)]
        x1d_loaded = [sem("x1d_loaded0"), sem("x1d_loaded1")]
        ea_loaded = [sem("ea_loaded0"), sem("ea_loaded1")]
        cmask_loaded = [sem("cmask_loaded0"), sem("cmask_loaded1")]
        ops_turned, opsT_copied = sem("ops_turned"), sem("opsT_copied")
        k_summed, q_summed, e_summed, v_summed = (sem(n) for n in ("k_summed", "q_summed", "e_summed", "v_summed"))
        k_biased, kq_made, kqe_made = sem("k_biased"), sem("kq_made"), sem("kqe_made")
        heads_summed, clipped, score_made = sem("heads_summed"), sem("clipped"), sem("score_made")
        weighed, cscanned, seg_turned = sem("weighed"), sem("cscanned"), sem("seg_turned")
        z_step, hc_made, yc_made = sem("z_step"), sem("hc_made"), sem("yc_made")
        cstats_step, croot_step, cnorm_ready = sem("cstats_step"), sem("croot_step"), sem("cnorm_ready")
        fin_made = sem("fin_made")
        out_scattered = [sem(f"out_scattered{j}") for j in range(EJ)]

        columns = [(mb1s, mb1), (gb1s, gb1), (ub1s, ub1), (mb2s, mb2), (bqs, bq), (bks, bk), (bes, be)]
        WEIGHTS = 16 * (18 + len(columns))

        def slot_total(slot):
            return 16 * len(range(slot, NGROUPS, 2))

        def node_rows(t, g):
            at = min(g * NROWS, N - NROWS) if isinstance(g, int) else g * NROWS
            return t[bass.DynSlice(at, NROWS), :].rearrange("(p j) f -> p (j f)", j=NJ)

        block = ctx.enter_context(nc.Block())

        @block.sync
        def _(sp):
            for to, of in ((ident, ident_c), (heads, heads_c), (mW1s, mW1), (gW1s, gW1), (mW2s, mW2),
                           (gW2c, gW2), (uW1x, uW1[0:D, :]), (uW1a, uW1[D:2 * D, :]),
                           (Wqs, Wq), (Wks, Wk), (Wes, We)):
                sp.dma_start(to[:], of).then_inc(weights_loaded, 16)
            sp.dma_start(uW2s[0:D, :], uW2).then_inc(weights_loaded, 16)
            sp.dma_start(uW2s[D:D + 1, :], ub2.rearrange("(a d) -> a d", a=1)).then_inc(weights_loaded, 16)
            for to, of in columns:
                sp.dma_start(to[:], of.rearrange("(d a) -> d a", a=1)).then_inc(weights_loaded, 16)
            sp.dma_start(gb2s[:], gb2.rearrange("(d a) -> d a", a=1).broadcast_to([D, 1])).then_inc(weights_loaded, 16)
            for to, of in ((lng, ln_g), (lnb, ln_b)):
                sp.dma_start(to[:], of.rearrange("(a d) -> a d", a=1).broadcast_to([P, D])).then_inc(weights_loaded, 16)
            sp.wait_ge(pads_set, 6)
            sp.dma_start(Wvs[:, 0:D], Wv).then_inc(weights_loaded, 16)
            sp.dma_start(bvs[0:D, :], bv.rearrange("(d a) -> d a", a=1)).then_inc(weights_loaded, 16)
            sp.dma_start(spare[:], spare_c).then_inc(index_loaded, 16)
            for to, of in ((src_i, src), (dst_i, dst)):
                sp.dma_start(to[:, 0:EFULL, :], of[0:EFULL * EROWS].rearrange("(g p j) -> p g j", p=P, j=EJ)).then_inc(index_loaded, 16)
                sp.dma_start(to[0:ETAIL_P, EFULL, :], of[EFULL * EROWS:E].rearrange("(p j) -> p j", j=EJ)).then_inc(index_loaded, 16)
            sp.dma_start(next_i[:, 0:EFULL, :], dst[1:EFULL * EROWS + 1].rearrange("(g p j) -> p g j", p=P, j=EJ)).then_inc(index_loaded, 16)
            sp.dma_start(next_i[0:ETAIL_P - 1, EFULL, :], dst[EFULL * EROWS + 1:E - EJ + 1].rearrange("(p j) -> p j", j=EJ)).then_inc(index_loaded, 16)
            sp.dma_start(next_i[ETAIL_P - 1:ETAIL_P, EFULL, 0:EJ - 1], dst[E - EJ + 1:E].rearrange("(a j) -> a j", a=1)).then_inc(index_loaded, 16)
            sp.dma_start(pre_d[N:N + EROWS, :].rearrange("(p j) f -> p (j f)", j=EJ), zeros[:]).then_inc(spare_zeroed, 16)
            sp.wait_ge(same_made, 1)
            sp.dma_start(cont_d[:, 0:1], zeros[0:1, 0:1]).then_inc(cont_stored, 16)
            sp.dma_start(cont_d[:, 1:1 + EGROUPS * EROWS].rearrange("a (g p j) -> (a p) g j", p=P, j=EJ), same[:]).then_inc(cont_stored, 16)

            def node_step(i, s, inner):
                if inner or i < NGROUPS:
                    if inner or i >= 2:
                        sp.wait_ge(x_turned, i - 1)
                    sp.dma_start(x_in[:, s, :], node_rows(x, i)).then_inc(x_loaded[s], 16)
                if inner or i >= 1:
                    sp.wait_ge(pre_copied, i)
                    if isinstance(i, int) and i == NGROUPS:
                        sp.wait_ge(pre_stored[s], slot_total(s))
                    sp.dma_start(node_rows(pre_d, i - 1), pre_io[:, 1 - s, :]).then_inc(pre_stored[1 - s], 16)

            sweep(sp, 0, NGROUPS + 1, 3, 4, node_step)

            sp.wait_ge(cont_stored, 32)

            def edge_step(i, s, inner):
                if inner or i >= 2:
                    sp.wait_ge(ein_turned, i - 1)
                    sp.wait_ge(scanned, i - 1)
                for j in range(EJ):
                    sp.wait_ge(xs_gathered[j], i * 16 + 16)
                sp.dma_start(ein[:, s, :, 0:D], rows[:, bass.DynSlice(i * EJ, EJ), :]).then_inc(ein_loaded[s], 16)
                if isinstance(i, int) and i == EFULL:
                    sp.dma_start(ein[0:ETAIL_P, s, :, D:D + DE], ea32[EFULL * EROWS:E, :].rearrange("(p j) f -> p j f", j=EJ)).then_inc(ein_loaded[s], 16)
                else:
                    sp.dma_start(ein[:, s, :, D:D + DE], ea32[bass.DynSlice(i * EROWS, EROWS), :].rearrange("(p j) f -> p j f", j=EJ)).then_inc(ein_loaded[s], 16)
                sp.dma_start(mask[0:D, s, :], cont_d[:, bass.DynSlice(i * EROWS, EROWS)].broadcast_to([D, EROWS])).then_inc(mask_loaded[s], 16)

            sweep(sp, 0, EGROUPS, 2, 1, edge_step)

            for j in range(EJ):
                sp.wait_ge(agg_added[j], 16 * EGROUPS)

            def update_step(i, s, inner):
                if inner or i < NGROUPS:
                    if inner or i >= 2:
                        sp.wait_ge(pre_turned, i - 1)
                    sp.dma_start(pre_io[:, s, :], node_rows(pre_d, i)).then_inc(pre_loaded[s], 16)
                    if inner or i >= 2:
                        sp.wait_ge(xb_made, i - 1)
                    sp.dma_start(x_in[:, s, :], node_rows(x, i)).then_inc(xn_loaded[s], 16)
                if inner or 3 <= i < NGROUPS + 3:
                    sp.wait_ge(x1_made, i - 2)
                    if isinstance(i, int) and i == NGROUPS + 2:
                        sp.wait_ge(x1_stored[s], slot_total(s))
                    sp.dma_start(node_rows(x1_d, i - 3), x1o[:, 1 - s, :]).then_inc(x1_stored[1 - s], 16)
                if inner or i >= 4:
                    sp.wait_ge(out_made, i - 3)
                    if isinstance(i, int) and i == NGROUPS + 3:
                        sp.wait_ge(out_stored[1 - s], slot_total(1 - s))
                    sp.dma_start(node_rows(out, i - 4), oo[:, s, :]).then_inc(out_stored[s], 16)

            sweep(sp, 0, NGROUPS + 4, 5, 6, update_step)

            def attend_step(i, s, inner):
                if inner or i >= 2:
                    sp.wait_ge(ops_turned, (i - 1) * 3)
                    sp.wait_ge(yc_made, i - 1)
                    sp.wait_ge(cscanned, i - 1)
                for j in range(EJ):
                    sp.wait_ge(xd_gathered[j], i * 16 + 16)
                sp.dma_start(x1d[:, s, :, :], rows[:, bass.DynSlice(i * EJ, EJ), :]).then_inc(x1d_loaded[s], 16)
                if isinstance(i, int) and i == EFULL:
                    sp.dma_start(ea[0:ETAIL_P, s, :, :], ea96[EFULL * EROWS:E, :].rearrange("(p j) f -> p j f", j=EJ)).then_inc(ea_loaded[s], 16)
                else:
                    sp.dma_start(ea[:, s, :, :], ea96[bass.DynSlice(i * EROWS, EROWS), :].rearrange("(p j) f -> p j f", j=EJ)).then_inc(ea_loaded[s], 16)
                sp.dma_start(mask[:, s, :], cont_d[:, bass.DynSlice(i * EROWS, EROWS)].broadcast_to([DH, EROWS])).then_inc(cmask_loaded[s], 16)

            sweep(sp, 0, EGROUPS, 2, 1, attend_step)
            for j in range(EJ):
                sp.wait_ge(out_scattered[j], 16 * EGROUPS)

        @block.gpsimd
        def _(pool):
            def rows_at(index, g, j):
                return bass.IndirectOffsetOnAxis(ap=index[:, g, j:j + 1], axis=0)

            pool.wait_ge(index_loaded, 16 * 8)
            pool.wait_ge(index_made, 3)
            for g in range(EGROUPS):
                for j in range(EJ):
                    if g >= 1:
                        pool.wait_ge(xs_gathered[j], 16 * g)
                    pool.indirect_dma_start(rows[:, g * EJ + j, :], None, x, rows_at(src_i, g, j)).then_inc(xs_gathered[j], 16)
            pool.wait_ge(spare_zeroed, 16)
            for s in range(2):
                pool.wait_ge(pre_stored[s], slot_total(s))
            for g in range(EGROUPS):
                pool.wait_ge(agg_copied, g + 1)
                for j in range(EJ):
                    if g >= 1:
                        pool.wait_ge(agg_added[j], 16 * g)
                    pool.indirect_dma_start(pre_d, rows_at(add_at, g, j), rows[:, g * EJ + j, :], None,
                                            bounds_check=N + EROWS - 1, oob_is_err=True,
                                            compute_op=ALU.add).then_inc(agg_added[j], 16)
            for s in range(2):
                pool.wait_ge(x1_stored[s], slot_total(s))
            for g in range(EGROUPS):
                for j in range(EJ):
                    pool.wait_ge(agg_added[j], 16 * EGROUPS)
                    if g >= 1:
                        pool.wait_ge(xd_gathered[j], 16 * g)
                    pool.indirect_dma_start(rows[:, g * EJ + j, :], None, x1_d, rows_at(dst_at, g, j)).then_inc(xd_gathered[j], 16)
            LAG = 3
            for g in range(EGROUPS + LAG):
                if g < EGROUPS:
                    if g >= 2:
                        pool.wait_ge(ops_turned, 3 * (g - 1))
                    for j in range(EJ):
                        if g >= 1:
                            pool.wait_ge(x1s_gathered[j], 16 * g)
                        pool.indirect_dma_start(x1s[:, g % 2, j, :], None, x1_d, rows_at(src_i, g, j)).then_inc(x1s_gathered[j], 16)
                b = g - LAG
                if b == 0:
                    for s in range(2):
                        pool.wait_ge(out_stored[s], slot_total(s))
                if b >= 0:
                    pool.wait_ge(fin_made, b + 1)
                    for j in range(EJ):
                        if b >= 1:
                            pool.wait_ge(out_scattered[j], 16 * b)
                        pool.indirect_dma_start(out, rows_at(put_at, b, j), fin[:, b % 2, j, :], None,
                                                bounds_check=N - 1, oob_is_err=False).then_inc(out_scattered[j], 16)

        @block.tensor
        def _(pe):
            pe.wait_ge(weights_loaded, WEIGHTS)
            pe.wait_ge(weights_made, 3)

            def turn(to, of, last=None):
                mmx = pe.transpose(to, of, ident[:, :])
                if last is not None:
                    mmx.then_inc(last, 1)

            def node_step(i, s, inner):
                if inner or i < NGROUPS:
                    pe.wait_ge(x_loaded[s], per_slot(i, s))
                    if inner or i >= 2:
                        pe.wait_ge(xT_copied, i - 1)
                    for j in range(NJ):
                        turn(ps[0:D, 2 * s + j // 4, (j % 4) * P:(j % 4 + 1) * P], x_in[:, s, j * D:(j + 1) * D],
                             x_turned if j == NJ - 1 else None)
                if inner or i >= 1:
                    pe.wait_ge(xT_copied, i)
                    if inner or i >= 3:
                        pe.wait_ge(pre_copied, i - 2)
                    for j in range(NJ):
                        m = pe.matmul(ps[:, 4 + 2 * (1 - s) + j // 4, (j % 4) * D:(j % 4 + 1) * D],
                                      nT[0:D, 1 - s, j * P:(j + 1) * P], uW1x[:, :], start=True, stop=True)
                    m.then_inc(pre_summed, 1)

            sweep(pe, 0, NGROUPS + 1, 3, 1, node_step)

            pe.wait_ge(xT_copied, NGROUPS)
            pe.wait_ge(pre_copied, NGROUPS)

            def edge_step(i, s, inner):
                if inner or 0 <= i < EGROUPS:
                    pe.wait_ge(einT_copied, i + 1)
                    if inner or i >= 1:
                        pe.wait_ge(gelu_done, i * 2)
                    pe.matmul(ps[0:D, 2, :], mW1s[:, :], einT[:, s, :], start=True, stop=True).then_inc(hidden_summed, 1)
                    pe.matmul(ps[0:D, 3, :], gW1s[:, :], einT[:, s, :], start=True, stop=True).then_inc(hidden_summed, 1)
                if inner or i + 1 < EGROUPS:
                    pe.wait_ge(ein_loaded[1 - s], (i + 1) * 16 + (32 - 16 * (1 - s)))
                    if inner or i >= 1:
                        pe.wait_ge(einT_copied, i)
                    to = ps[:, 1 - s, :].rearrange("p (c j) -> p j c", j=EJ)
                    for j in range(EJ):
                        turn(to[:, j, :], ein[:, 1 - s, j, :], ein_turned if j == EJ - 1 else None)
                if inner or i >= 1:
                    pe.wait_ge(scanned, i)
                    if inner or i >= 3:
                        pe.wait_ge(agg_copied, i - 2)
                    of = seg[0:D, 1 - s, :].rearrange("p (c j) -> p j c", j=EJ)
                    for j in range(EJ):
                        m = pe.matmul(ps[:, 6 + (1 - s), j * D:(j + 1) * D], of[:, j, :], uW1a[:, :], start=True, stop=True)
                    m.then_inc(agg_summed, 1)
                if inner or 0 <= i < EGROUPS:
                    pe.wait_ge(gelu_done, i * 2 + 1)
                    if inner or i >= 1:
                        pe.wait_ge(gated, i)
                    pe.matmul(ps[0:D, 4, :], mW2s[:, :], gm[:, :], start=True, stop=True).then_inc(message_summed, 1)
                    pe.wait_ge(gelu_done, i * 2 + 2)
                    if inner or i >= 1:
                        pe.wait_ge(tanh_done, i)
                    pe.matmul(ps[0:D, 5, :], gW2s[:, :], gg[:, :], start=True, stop=True).then_inc(gate_summed, 1)

            sweep(pe, -1, EGROUPS + 1, 4, 2, edge_step)

            pe.wait_ge(einT_copied, EGROUPS)
            pe.wait_ge(gelu_done, 2 * EGROUPS)
            pe.wait_ge(gated, EGROUPS)
            pe.wait_ge(tanh_done, EGROUPS)
            pe.wait_ge(agg_copied, EGROUPS)

            def update_step(i, s, inner):
                if inner or i < NGROUPS:
                    pe.wait_ge(pre_loaded[s], per_slot(i, s))
                    if inner or i >= 2:
                        pe.wait_ge(node_gelu, i - 1)
                    for j in range(NJ):
                        turn(ps[0:D, 2 * s + j // 4, (j % 4) * P:(j % 4 + 1) * P], pre_io[:, s, j * D:(j + 1) * D],
                             pre_turned if j == NJ - 1 else None)
                if inner or i >= 1:
                    pe.wait_ge(node_gelu, i)
                    if inner or i >= 3:
                        pe.wait_ge(h_made, i - 2)
                    for j in range(NJ):
                        m = pe.matmul(ps[:, 4 + 2 * (1 - s) + j // 4, (j % 4) * D:(j % 4 + 1) * D],
                                      nT[:, 1 - s, j * P:(j + 1) * P], uW2s[:, :], start=True, stop=True)
                    m.then_inc(update_summed, 1)

            sweep(pe, 0, NGROUPS + 1, 3, 1, update_step)

            pe.wait_ge(node_gelu, NGROUPS)
            pe.wait_ge(h_made, NGROUPS)

            def attend_step(i, s, inner):
                if inner or 0 <= i < EGROUPS:
                    pe.wait_ge(opsT_copied, i * 3 + 3)
                    xsT, xdT, eaT = opT[s]
                    if inner or i >= 1:
                        pe.wait_ge(k_biased, i)
                    pe.matmul(ps[0:D, 3, :], Wks[:, :], xsT, start=True, stop=True).then_inc(k_summed, 1)
                    if inner or i >= 1:
                        pe.wait_ge(kq_made, i)
                    pe.matmul(ps[0:D, 4, :], Wqs[:, :], xdT, start=True, stop=True).then_inc(q_summed, 1)
                    if inner or i >= 1:
                        pe.wait_ge(clipped, i)
                    pe.matmul(ps[0:D, 5, :], Wes[:, :], eaT, start=True, stop=True).then_inc(e_summed, 1)
                    if inner or i >= 1:
                        pe.wait_ge(weighed, i)
                    pe.matmul(ps[0:DH, 6, :], Wvs[:, :], xsT, start=True, stop=True).then_inc(v_summed, 1)
                if inner or i >= 1:
                    pe.wait_ge(cscanned, i)
                    if inner or i >= 2:
                        pe.wait_ge(hc_made, i - 1)
                    of = seg[:, 1 - s, :].rearrange("p (c j) -> p j c", j=EJ)
                    for j in range(EJ):
                        m = pe.transpose(ps[:, 7, j * DH:(j + 1) * DH], of[:, j, :], ident[0:DH, 0:DH])
                    m.then_inc(seg_turned, 1)
                if inner or i + 1 < EGROUPS:
                    for j in range(EJ):
                        pe.wait_ge(x1s_gathered[j], i * 16 + 32)
                    pe.wait_ge(x1d_loaded[1 - s], per_slot(i + 1, 1 - s))
                    pe.wait_ge(ea_loaded[1 - s], per_slot(i + 1, 1 - s))
                    if inner or i >= 0:
                        pe.wait_ge(opsT_copied, i * 3 + 3)
                    for b, of in enumerate((x1s, x1d, ea)):
                        to = ps[0:D, b, :].rearrange("p (c j) -> p j c", j=EJ)
                        for j in range(EJ):
                            turn(to[:, j, :], of[:, 1 - s, j, :], ops_turned if j == EJ - 1 else None)
                if inner or 0 <= i < EGROUPS:
                    pe.wait_ge(kqe_made, i + 1)
                    pe.matmul(ps[0:DH, 5, :], heads[:, :], kqe[:, :], start=True, stop=True).then_inc(heads_summed, 1)

            sweep(pe, -1, EGROUPS + 1, 4, 2, attend_step)

        @block.scalar
        def _(act):
            act.wait_ge(weights_loaded, WEIGHTS)
            act.wait_ge(weights_made, 5)

            def node_step(i, s, inner):
                act.wait_ge(x_turned, i + 1)
                if inner or i >= 2:
                    act.wait_ge(pre_summed, i - 1)
                act.activation(nT[0:D, s, :].rearrange("p (b c) -> p b c", b=2), ps[0:D, 2 * s:2 * s + 2, :], ACT.Copy).then_inc(xT_copied, 1)

            sweep(act, 0, NGROUPS, 3, 0, node_step)

            def edge_step(i, s, inner):
                if inner or i >= 0:
                    act.wait_ge(hidden_summed, i * 2 + 1)
                    if inner or i >= 1:
                        act.wait_ge(message_summed, i)
                    act.activation(gm[:, :], ps[0:D, 2, :], ACT.Gelu, bias=mb1s[:, 0:1]).then_inc(gelu_done, 1)
                    act.wait_ge(hidden_summed, i * 2 + 2)
                    if inner or i >= 1:
                        act.wait_ge(gate_summed, i)
                    act.activation(gg[:, :], ps[0:D, 3, :], ACT.Gelu, bias=gb1s[:, 0:1]).then_inc(gelu_done, 1)
                if inner or i + 1 < EGROUPS:
                    act.wait_ge(ein_turned, i + 2)
                    if inner or i >= 1:
                        act.wait_ge(hidden_summed, i * 2)
                    act.activation(einT[:, 1 - s, :], ps[:, 1 - s, :], ACT.Copy).then_inc(einT_copied, 1)
                if inner or i >= 0:
                    act.wait_ge(gate_summed, i + 1)
                    if inner or i >= 1:
                        act.wait_ge(gated, i)
                    act.activation(gate[:, :], ps[0:D, 5, :], ACT.Tanh, bias=gb2s[:, 0:1], scale=0.5).then_inc(tanh_done, 1)

            sweep(act, -1, EGROUPS, 4, 1, edge_step)

            def update_step(i, s, inner):
                if inner or i < NGROUPS:
                    act.wait_ge(pre_turned, i + 1)
                    if inner or i >= 2:
                        act.wait_ge(update_summed, i - 1)
                    act.activation(nT[0:D, s, :].rearrange("p (b c) -> p b c", b=2), ps[0:D, 2 * s:2 * s + 2, :], ACT.Gelu, bias=ub1s[:, 0:1]).then_inc(node_gelu, 1)
                if inner or i >= 1:
                    act.wait_ge(norms_ready, i)
                k = s
                if inner or 1 <= i < NGROUPS + 1:
                    for j in range(NJ):
                        t = h[:, 1 - s, j * D:(j + 1) * D]
                        z = act.activation(t, t, ACT.Identity, bias=nshift[:, k, 0, j:j + 1], scale=nscale[:, k, 0, j:j + 1])
                    z.then_inc(z_made, 1)
                if inner or 2 <= i < NGROUPS + 2:
                    if inner or i >= 4:
                        act.wait_ge(x1_stored[s], per_slot(i - 4, s))
                        act.wait_ge(out_made, i - 3)
                    for j in range(NJ):
                        o = act.activation(x1o[:, s, j * D:(j + 1) * D], y[:, s, j * D:(j + 1) * D], ACT.Identity,
                                           bias=nshift[:, k, 1, j:j + 1], scale=nscale[:, k, 1, j:j + 1])
                    o.then_inc(x1_made, 1)
                if inner or i >= 3:
                    if inner or i >= 5:
                        act.wait_ge(out_stored[1 - s], per_slot(i - 5, 1 - s))
                    act.wait_ge(x1_made, i - 2)
                    for j in range(NJ):
                        o = act.activation(oo[:, 1 - s, j * D:(j + 1) * D], x1o[:, 1 - s, j * D:(j + 1) * D], ACT.Identity,
                                           scale=nscale[:, k, 2, j:j + 1])
                    o.then_inc(out_made, 1)

            sweep(act, 0, NGROUPS + 3, 5, 4, update_step)

            def attend_step(i, s, inner):
                if inner or 0 <= i < EGROUPS:
                    act.wait_ge(k_summed, i + 1)
                    if inner or i >= 1:
                        act.wait_ge(kq_made, i)
                    act.activation(kS[:, :], ps[0:D, 3, :], ACT.Identity, bias=bks[:, 0:1]).then_inc(k_biased, 1)
                if inner or i + 1 < EGROUPS:
                    for b in range(3):
                        act.wait_ge(ops_turned, i * 3 + 4 + b)
                        if b == 0 and (inner or i >= 1):
                            act.wait_ge(v_summed, i)
                            act.wait_ge(e_summed, i)
                            act.wait_ge(q_summed, i)
                        act.activation(opT[1 - s][b], ps[0:D, b, :], ACT.Copy).then_inc(opsT_copied, 1)
                if inner or 0 <= i < EGROUPS:
                    act.wait_ge(clipped, i + 1)
                    if inner or i >= 1:
                        act.wait_ge(weighed, i)
                    act.activation(score[:, :], clip[:, :], ACT.Exp).then_inc(score_made, 1)
                if inner or i >= 1:
                    act.wait_ge(cnorm_ready, i)
                    if inner or i >= 3:
                        for j in range(EJ):
                            act.wait_ge(out_scattered[j], i * 16 - 32)
                    for j in range(EJ):
                        o = act.activation(fin[:, 1 - s, j, :], yc[:, 1 - s, j, :], ACT.Identity,
                                           bias=cshift[:, 1 - s, j:j + 1], scale=cscale[:, 1 - s, j:j + 1])
                    o.then_inc(fin_made, 1)

            sweep(act, -1, EGROUPS + 1, 5, 2, attend_step)

        @block.vector
        def _(dve):
            dve.memset(src_i[:, EFULL, :], 0).then_inc(pads_set, 1)
            dve.memset(dst_i[:, EFULL, :], FAR).then_inc(pads_set, 1)
            dve.memset(next_i[:, EFULL, :], FAR).then_inc(pads_set, 1)
            dve.memset(zeros[:, :], 0.0).then_inc(pads_set, 1)
            dve.memset(Wvs[:, :], 0.0).then_inc(pads_set, 1)
            dve.memset(bvs[:, :], 1.0).then_inc(pads_set, 1)
            dve.memset(nT[D:D + 1, :, :], 1.0).then_inc(weights_made, 1)
            dve.wait_ge(index_loaded, 16 * 8)
            dve.tensor_tensor(same[:, :, :], dst_i[:, :, :], next_i[:, :, :], ALU.is_equal).then_inc(same_made, 1)
            dve.tensor_tensor(shift[:, :, :], spare[:, :].unsqueeze(1).broadcast_to([P, EGROUPS, EJ]), dst_i[:, :, :], ALU.subtract).then_inc(same_made, 1)
            dve.tensor_scalar(dst_at[:, :, :], dst_i[:, :, :], N - 1, None, ALU.min).then_inc(index_made, 1)
            dve.wait_ge(same_made, 2)
            dve.tensor_tensor(shift[:, :, :], shift[:, :, :], same[:, :, :], ALU.mult).then_inc(same_made, 1)
            dve.scalar_tensor_tensor(put_at[:, :, :], same[:, :, :], float(FAR), dst_i[:, :, :], ALU.mult, ALU.add).then_inc(index_made, 1)
            dve.wait_ge(same_made, 3)
            dve.tensor_tensor(add_at[:, :, :], dst_i[:, :, :], shift[:, :, :], ALU.add).then_inc(index_made, 1)
            dve.wait_ge(pads_set, 6)
            dve.wait_ge(weights_loaded, WEIGHTS)
            dve.tensor_scalar(gW2s[:, :], zeros[0:D, 0:D], gW2c[:, 0:1], None, ALU.add).then_inc(weights_made, 1)
            dve.tensor_scalar(mW2s[:, :], mW2s[:, :], 0.5, None, ALU.mult).then_inc(weights_made, 1)
            dve.tensor_scalar(mb2s[:, :], mb2s[:, :], 0.5, None, ALU.mult).then_inc(weights_made, 1)
            dve.tensor_scalar(gb2s[:, :], gb2s[:, :], 0.5, None, ALU.mult).then_inc(weights_made, 1)

            def node_step(i, s, inner):
                dve.wait_ge(pre_summed, i + 1)
                if inner or i >= 2:
                    dve.wait_ge(pre_stored[s], per_slot(i - 2, s))
                dve.tensor_copy(pre_io[:, s, :].rearrange("p (b c) -> p b c", b=2), two_banks(4 + 2 * s)).then_inc(pre_copied, 1)

            sweep(dve, 0, NGROUPS, 3, 0, node_step)
            dve.wait_ge(weights_made, 5)

            def edge_step(i, s, inner):
                if inner or i >= 1:
                    dve.wait_ge(agg_summed, i)
                    dve.tensor_copy(rows[:, bass.DynSlice(i * EJ - EJ, EJ), :],
                                    ps[:, 6 + (1 - s), 0:EJ * D].rearrange("p (j f) -> p j f", j=EJ)).then_inc(agg_copied, 1)
                if inner or i < EGROUPS:
                    dve.wait_ge(tanh_done, i + 1)
                    dve.tensor_scalar(gate[:, :], gate[:, :], 1.0, None, ALU.add).then_inc(gate_done, 1)
                    dve.wait_ge(gate_done, i + 1)
                    dve.wait_ge(message_summed, i + 1)
                    dve.scalar_tensor_tensor(mm[:, :], ps[0:D, 4, :], mb2s[:, 0:1], gate[:, :], ALU.add, ALU.mult).then_inc(gated, 1)
                    dve.wait_ge(gated, i + 1)
                    dve.wait_ge(mask_loaded[s], per_slot(i, s))
                    if inner or i >= 2:
                        dve.wait_ge(agg_summed, i - 1)
                    if inner or i >= 1:
                        dve.wait_ge(scanned, i)
                    before = seg[0:D, 1 - s, EROWS - 1:EROWS] if inner or i >= 1 else 0.0
                    dve.tensor_tensor_scan(seg[0:D, s, :], mask[0:D, s, :], mm[:, :], before, ALU.mult, ALU.add).then_inc(scanned, 1)

            sweep(dve, 0, EGROUPS + 1, 3, 1, edge_step)

            lngb = lng[:, :].unsqueeze(1).broadcast_to([P, NJ, D])
            lnbb = lnb[:, :].unsqueeze(1).broadcast_to([P, NJ, D])

            def rows_of(t, s):
                return t[:, s, :].rearrange("p (j f) -> p j f", j=NJ)

            def combine(stats, total, apart, squares, var, done, count):
                dve.tensor_tensor(total, stats(1), stats(4), ALU.add).then_inc(done, 1)
                dve.tensor_tensor(apart, stats(1), stats(4), ALU.subtract).then_inc(done, 1)
                dve.tensor_tensor(squares, stats(2), stats(5), ALU.add).then_inc(done, 1)
                dve.wait_ge(done, count + 2)
                dve.scalar_tensor_tensor(apart, apart, 0.25, apart, ALU.mult, ALU.mult).then_inc(done, 1)
                dve.wait_ge(done, count + 4)
                dve.scalar_tensor_tensor(var, squares, 1.0 / D, apart, ALU.mult, ALU.add).then_inc(done, 1)
                dve.wait_ge(done, count + 5)

            def root(var, guess, half, done, count):
                gi, vi = guess.bitcast(I32), var.bitcast(I32)
                dve.tensor_scalar(gi, vi, 1, None, ALU.arith_shift_right).then_inc(done, 1)
                dve.wait_ge(done, count + 1)
                dve.tensor_scalar(gi, gi, -1, MAGIC, ALU.mult, ALU.add).then_inc(done, 1)
                for k in range(3):
                    dve.wait_ge(done, count + 2 + 3 * k)
                    dve.scalar_tensor_tensor(half, guess, -0.5, guess, ALU.mult, ALU.mult).then_inc(done, 1)
                    dve.wait_ge(done, count + 3 + 3 * k)
                    dve.tensor_tensor(half, half, var, ALU.mult).then_inc(done, 1)
                    dve.wait_ge(done, count + 4 + 3 * k)
                    dve.scalar_tensor_tensor(guess, half, 1.5, guess, ALU.add, ALU.mult).then_inc(done, 1)
                dve.wait_ge(done, count + 11)

            dve.memset(bn[:, :, :, :], 1.0).then_inc(stats_step, 1)
            dve.memset(nv[:, :, :], 1.0).then_inc(stats_step, 1)
            dve.wait_ge(stats_step, 2)
            flat = lambda t: t[:, :, :].rearrange("p a j -> p (a j)")
            NSTEPS = 5 + 1 + 11 + 3

            def update_step(i, s, inner):
                n = (i - 1)
                if inner or i < NGROUPS + 1:
                    dve.wait_ge(update_summed, i)
                    dve.wait_ge(xn_loaded[1 - s], per_slot(i - 1, 1 - s))
                    if inner or i >= 3:
                        dve.wait_ge(zg_made, i - 2)
                        dve.wait_ge(y_made, i - 2)
                    dve.tensor_tensor(h[:, 1 - s, :].rearrange("p (b c) -> p b c", b=2), two_banks(4 + 2 * (1 - s)),
                                      x_in[:, 1 - s, :].rearrange("p (b c) -> p b c", b=2), ALU.add).then_inc(h_made, 1)
                    dve.tensor_tensor(rows_of(xb, 1 - s), rows_of(x_in, 1 - s), lnbb, ALU.add).then_inc(xb_made, 1)
                    dve.wait_ge(h_made, i)
                    for j in range(NJ):
                        b = dve.bn_stats(bn[:, 0, j, :], h[:, 1 - s, j * D:(j + 1) * D])
                    b.then_inc(h_measured, 1)
                if inner or 2 <= i < NGROUPS + 2:
                    dve.wait_ge(z_made, i - 1)
                    dve.tensor_tensor(rows_of(h, s), rows_of(h, s), lngb, ALU.mult).then_inc(zg_made, 1)
                    if inner or i >= 4:
                        dve.wait_ge(x1_made, i - 3)
                    dve.wait_ge(zg_made, i - 1)
                    dve.wait_ge(xb_made, i - 1)
                    dve.tensor_tensor(y[:, s, :], h[:, s, :], xb[:, s, :], ALU.add).then_inc(y_made, 1)
                    dve.wait_ge(y_made, i - 1)
                    for j in range(NJ):
                        b = dve.bn_stats(bn[:, 1, j, :], y[:, s, j * D:(j + 1) * D])
                    b.then_inc(y_measured, 1)
                    dve.wait_ge(y_measured, i - 1)
                if inner or i < NGROUPS + 1:
                    dve.wait_ge(h_measured, i)
                combine(lambda k: bn[:, :, :, k], msum[:, :, :], mdif[:, :, :], sqs[:, :, :], nv[:, 0:2, :], root_step, n * NSTEPS)
                dve.tensor_scalar(nvar[:, :, :], nv[:, :, :], EPS, None, ALU.add).then_inc(root_step, 1)
                dve.wait_ge(root_step, n * NSTEPS + 6)
                root(flat(nvar), flat(nroot), flat(nhalf), root_step, n * NSTEPS + 6)
                if inner or i >= 3:
                    if inner or i < NGROUPS + 3:
                        dve.wait_ge(z_made, i - 2)
                    if inner or i >= 4:
                        dve.wait_ge(x1_made, i - 3)
                    if inner or i >= 5:
                        dve.wait_ge(out_made, i - 4)
                dve.scalar_tensor_tensor(nshift[:, s, :, :], msum[:, :, :], -0.5, nroot[:, 0:2, :], ALU.mult, ALU.mult).then_inc(root_step, 1)
                dve.wait_ge(root_step, n * NSTEPS + 18)
                dve.tensor_copy(nscale[:, s, :, :], nroot[:, :, :]).then_inc(norms_ready, 1)
                dve.tensor_tensor(nv[:, 2, :], nv[:, 1, :], nroot[:, 1, :], ALU.mult).then_inc(root_step, 1)
                dve.wait_ge(root_step, n * NSTEPS + 19)
                dve.tensor_tensor(nv[:, 2, :], nv[:, 2, :], nroot[:, 1, :], ALU.mult).then_inc(root_step, 1)
                dve.wait_ge(root_step, n * NSTEPS + 20)

            sweep(dve, 1, NGROUPS + 3, 5, 4, update_step)

            def attend_step(i, s, inner):
                if inner or i < EGROUPS:
                    dve.wait_ge(q_summed, i + 1)
                    dve.wait_ge(k_biased, i + 1)
                    dve.scalar_tensor_tensor(kq[:, :], ps[0:D, 4, :], bqs[:, 0:1], kS[:, :], ALU.add, ALU.mult).then_inc(kq_made, 1)
                    dve.wait_ge(e_summed, i + 1)
                    dve.wait_ge(kq_made, i + 1)
                    if inner or i >= 1:
                        dve.wait_ge(heads_summed, i)
                    dve.scalar_tensor_tensor(kqe[:, :], ps[0:D, 5, :], bes[:, 0:1], kq[:, :], ALU.add, ALU.mult).then_inc(kqe_made, 1)
                if inner or i >= 1:
                    dve.wait_ge(seg_turned, i)
                    back = ps[:, 7, 0:EJ * DH].rearrange("p (j f) -> p j f", j=EJ)
                    dve.tensor_scalar(zr[:, 0, :, :], back[:, :, D:DH], 1e-6, None, ALU.add).then_inc(z_step, 1)
                    dve.wait_ge(z_step, i * 2 - 1)
                    dve.reciprocal(zr[:, 1, :, :], zr[:, 0, :, :]).then_inc(z_step, 1)
                    dve.wait_ge(z_step, i * 2)
                    for j in range(EJ):
                        b = dve.tensor_tensor(hc[:, j, :].rearrange("p (a d) -> p a d", a=HEADS),
                                              back[:, j, 0:D].rearrange("p (a d) -> p a d", a=HEADS),
                                              zr[:, 1, j, :].unsqueeze(2).broadcast_to([P, HEADS, HD]), ALU.mult)
                    b.then_inc(hc_made, 1)
                    dve.wait_ge(hc_made, i)
                    dve.wait_ge(x1d_loaded[1 - s], per_slot(i - 1, 1 - s))
                    if inner or i >= 3:
                        dve.wait_ge(fin_made, i - 2)
                    dve.tensor_tensor(yc[:, 1 - s, :, :], hc[:, :, :], x1d[:, 1 - s, :, :], ALU.add).then_inc(yc_made, 1)
                if inner or i < EGROUPS:
                    dve.wait_ge(heads_summed, i + 1)
                    if inner or i >= 1:
                        dve.wait_ge(score_made, i)
                    dve.tensor_scalar(clip[:, :], ps[0:DH, 5, :], -5.0, 5.0, ALU.max, ALU.min).then_inc(clipped, 1)
                if inner or i < EGROUPS:
                    dve.wait_ge(score_made, i + 1)
                    dve.wait_ge(v_summed, i + 1)
                    dve.scalar_tensor_tensor(msg[:, :], ps[0:DH, 6, :], bvs[:, 0:1], score[:, :], ALU.add, ALU.mult).then_inc(weighed, 1)
                if inner or i >= 1:
                    dve.wait_ge(yc_made, i)
                    for j in range(EJ):
                        b = dve.bn_stats(cbn[:, j, :], yc[:, 1 - s, j, :])
                    b.then_inc(cstats_step, 1)
                if inner or i < EGROUPS:
                    dve.wait_ge(weighed, i + 1)
                    dve.wait_ge(cmask_loaded[s], per_slot(i, s))
                    if inner or i >= 2:
                        dve.wait_ge(seg_turned, i - 1)
                    if inner or i >= 1:
                        dve.wait_ge(cscanned, i)
                    before = seg[:, 1 - s, EROWS - 1:EROWS] if inner or i >= 1 else 0.0
                    dve.tensor_tensor_scan(seg[:, s, :], mask[:, s, :], msg[:, :], before, ALU.mult, ALU.add).then_inc(cscanned, 1)
                if inner or i >= 1:
                    dve.wait_ge(cstats_step, i)
                    combine(lambda k: cbn[:, :, k], csum[:, :], cdif[:, :], csqs[:, :], cv[:, :], croot_step, i * 18 - 18)
                    dve.tensor_scalar(cvar[:, :], cv[:, :], EPS, None, ALU.add).then_inc(croot_step, 1)
                    dve.wait_ge(croot_step, i * 18 - 12)
                    root(cvar[:, :], croot[:, :], chalf[:, :], croot_step, i * 18 - 12)
                    dve.tensor_copy(cscale[:, 1 - s, :], croot[:, :]).then_inc(croot_step, 1)
                    dve.wait_ge(croot_step, i * 18)
                    dve.scalar_tensor_tensor(cshift[:, 1 - s, :], csum[:, :], -0.5, croot[:, :], ALU.mult, ALU.mult).then_inc(cnorm_ready, 1)

            sweep(dve, 0, EGROUPS + 1, 4, 2, attend_step)


_RENAMED = {"edge_attr_32": "ea32", "edge_attr_96": "ea96"}
_ORDER = ["x", "src", "dst", "edge_attr_32", "edge_attr_96"] + [
    f"L0_gnn_{n}" for n in ("mW1", "mb1", "mW2", "mb2", "gW1", "gb1", "gW2", "gb2", "uW1", "ub1", "uW2", "ub2", "ln_g", "ln_b")] + [
    f"L1_gnn_{n}" for n in ("Wq", "bq", "Wk", "bk", "We", "be", "Wv", "bv")]


def shape_constants():
    heads = np.zeros((D, DH), np.float32)
    for f in range(D):
        heads[f, f // HD * HD:(f // HD + 1) * HD] = HD ** -0.5
        heads[f, D + f // HD] = HD ** -0.5
    spare = (N + np.arange(P)[:, None] + P * np.arange(EJ)[None, :]).astype(np.int32)
    return {"ident_c": np.eye(P, dtype=np.float32), "heads_c": heads, "spare_c": spare}


def kernel(**inputs):
    import concourse.bacc as bacc
    from concourse.bass_utils import run_bass_kernel_spmd

    nc = bacc.Bacc("TRN2", target_bir_lowering=False, num_devices=1)
    arrays = {f"in_{n}": np.ascontiguousarray(inputs[n]) for n in _ORDER} | shape_constants()
    args = [nc.dram_tensor(n, a.shape, mybir.dt.from_np(a.dtype), kind="ExternalInput").ap() for n, a in arrays.items()]
    out = nc.dram_tensor("out", [N, D], F32, kind="ExternalOutput").ap()
    build(nc, *args, out)
    return run_bass_kernel_spmd(nc, [arrays], core_ids=[0]).results[0]["out"]
```

```python
from contextlib import ExitStack

import numpy as np

import concourse.bass as bass
from concourse import mybir

P = 128
N, E, D, DE = 50000, 25000, 96, 32
HEADS = 8
HD = D // HEADS
DH = D + HEADS
EJ = 4
EROWS = P * EJ
EGROUPS = -(-E // EROWS)
EFULL = EGROUPS - 1
ETAIL_P = (E - EFULL * EROWS) // EJ
NJ = 8
NROWS = P * NJ
NGROUPS = -(-N // NROWS)
FAR = 1 << 20
BANK = 512
MAGIC = 0x5F3759DF
EPS = 1e-5

F32 = mybir.dt.float32
I32 = mybir.dt.int32
ALU = mybir.AluOpType
ACT = mybir.ActivationFunctionType

assert E % EJ == 0 and EGROUPS == NGROUPS


def sweep(eng, start, stop, front, back, step):
    first, last = start + front, stop - back
    last -= (last - first) % 2
    for i in range(start, first):
        step(i, i % 2, False)
    with eng.Fori(first, last - 1, 2) as i:
        step(i, first % 2, True)
        step(i + 1, (first + 1) % 2, True)
    for i in range(last, stop):
        step(i, i % 2, False)


def per_slot(i, slot):
    return i * 8 + (16 - 8 * slot)


def build(nc, x, src, dst, ea32, ea96, mW1, mb1, mW2, mb2, gW1, gb1, gW2, gb2, uW1, ub1, uW2, ub2,
          ln_g, ln_b, Wq, bq, Wk, bk, We, be, Wv, bv, ident_c, heads_c, spare_c, bounds_c, out):
    with ExitStack() as ctx:
        def sb(name, shape, dt=F32):
            return ctx.enter_context(nc.sbuf_tensor(name, shape, dt))

        def sem(name):
            return ctx.enter_context(nc.semaphore(name))

        pre_d = nc.dram_tensor("pre_d", [N + EROWS, D], F32).ap()
        x1_d = pre_d[0:N, :]
        cont_d = nc.dram_tensor("cont_d", [1, EGROUPS * EROWS + EJ], F32).ap()

        ident = sb("ident", [P, P])
        heads = sb("heads", [D, DH])
        mW1s, gW1s = sb("mW1s", [P, D]), sb("gW1s", [P, D])
        mW2s, gW2c, gW2s = sb("mW2s", [D, D]), sb("gW2c", [D, 1]), sb("gW2s", [D, D])
        uW1x, uW1a, uW2s = sb("uW1x", [D, D]), sb("uW1a", [D, D]), sb("uW2s", [D + 1, D])
        Wqs, Wks, Wes, Wvs = sb("Wqs", [D, D]), sb("Wks", [D, D]), sb("Wes", [D, D]), sb("Wvs", [D, DH])
        mb1s, gb1s, mb2s, gb2s, ub1s = (sb(n, [D, 1]) for n in ("mb1s", "gb1s", "mb2s", "gb2s", "ub1s"))
        bqs, bks, bes, bvs = sb("bqs", [D, 1]), sb("bks", [D, 1]), sb("bes", [D, 1]), sb("bvs", [DH, 1])
        lng, lnb = sb("lng", [P, D]), sb("lnb", [P, D])
        zeros = sb("zeros", [P, EJ * D])
        src_i, dst_i, next_i = (sb(n, [P, EGROUPS, EJ], I32) for n in ("src_i", "dst_i", "next_i"))
        spare = sb("spare", [P, EJ], I32)
        group_dst = sb("group_dst", [1, EGROUPS + 1], I32)
        bounds = sb("bounds", [1, 2, NGROUPS], I32)
        counts = sb("counts", [1, 2, EGROUPS])
        pairs = sb("pairs", [1, 2, EGROUPS], I32)
        need_agg = sb("need_agg", [1, NGROUPS], I32)
        need_x1 = sb("need_x1", [1, 2, EGROUPS], I32)
        same = sb("same", [P, EGROUPS, EJ])
        shift = sb("shift", [P, EGROUPS, EJ])
        add_at = sb("add_at", [P, EGROUPS, EJ], I32)
        put_at = sb("put_at", [P, EGROUPS, EJ], I32)
        dst_at = sb("dst_at", [P, EGROUPS, EJ], I32)
        rows = sb("rows", [P, EGROUPS * EJ, D])
        below = rows[0:1, :, :].rearrange("a r f -> a (r f)")[:, 0:EGROUPS * NGROUPS].rearrange("a (e n) -> a e n", e=EGROUPS)

        x_in = sb("x_in", [P, 2, NJ * D])
        pre_io = sb("pre_io", [P, 2, NJ * D])
        nT = sb("nT", [D + 1, 2, NJ * P])
        h, z, xb, y = (sb(n, [P, 2, NJ * D]) for n in ("h", "z", "xb", "y"))
        x1o, oo = sb("x1o", [P, 2, NJ * D]), sb("oo", [P, 2, NJ * D])
        bn = sb("bn", [P, 2, NJ, 6])
        msum, mdif, sqs, nv = (sb(n, [P, k, NJ]) for n, k in (("msum", 2), ("mdif", 2), ("sqs", 2), ("nv", 3)))
        nvar, nroot, nhalf = sb("nvar", [P, 3, NJ]), sb("nroot", [P, 3, NJ]), sb("nhalf", [P, 3, NJ])
        nscale, nshift = sb("nscale", [P, 2, 3, NJ]), sb("nshift", [P, 2, 2, NJ])

        ein = sb("ein", [P, 2, EJ, D + DE])
        einT = sb("einT", [P, 2, EROWS])
        hidden = [sb(n, [DH, EROWS]) for n in ("hidden0", "hidden1", "hidden2", "hidden3")]
        gm, gg, gate, mm = (t[0:D, :] for t in hidden)
        mask = sb("mask", [DH, 2, EROWS])
        seg = sb("seg", [DH, 2, EROWS])

        x1s = sb("x1s", [P, 2, EJ, D])
        x1d = sb("x1d", [P, 2, EJ, D])
        ea = sb("ea", [P, 2, EJ, D])
        kS, kq, kqe = (t[0:D, :] for t in hidden[0:3])
        clip = hidden[3]
        score, msg = (sb(n, [DH, EROWS]) for n in ("score", "msg"))
        yc, fin = sb("yc", [P, 2, EJ, D]), sb("fin", [P, 2, EJ, D])
        hc = sb("hc", [P, EJ, D])
        zr = sb("zr", [P, 2, EJ, HEADS])
        cbn = sb("cbn", [P, EJ, 6])
        csum, cdif, csqs, cv = (sb(n, [P, EJ]) for n in ("csum", "cdif", "csqs", "cv"))
        cvar, croot, chalf = sb("cvar", [P, EJ]), sb("croot", [P, EJ]), sb("chalf", [P, EJ])
        cscale, cshift = sb("cscale", [P, 2, EJ]), sb("cshift", [P, 2, EJ])

        ps = ctx.enter_context(nc.psum_tensor("ps", [P, 8, BANK], F32))

        def two_banks(b):
            return ps[:, b:b + 2, 0:EJ * D]

        nTf = nT[0:D, :, :].rearrange("p s c -> p (s c)")
        opT = [[nTf[:, 0:512], nTf[:, 512:1024], nTf[:, 1024:1536]],
               [nTf[:, 1536:2048], einT[0:D, 0, :], einT[0:D, 1, :]]]

        pads_set = sem("pads_set")
        weights_loaded, index_loaded = sem("weights_loaded"), sem("index_loaded")
        index_made, same_made, cont_stored = sem("index_made"), sem("same_made"), sem("cont_stored")
        needs_step, needs_made = sem("needs_step"), sem("needs_made")
        weights_made, spare_zeroed = sem("weights_made"), sem("spare_zeroed")
        x_loaded = [sem("x_loaded0"), sem("x_loaded1")]
        x_turned, xT_copied = sem("x_turned"), sem("xT_copied")
        pre_summed, pre_copied = sem("pre_summed"), sem("pre_copied")
        pre_stored = [sem("pre_stored0"), sem("pre_stored1")]
        xs_gathered = [sem(f"xs_gathered{j}") for j in range(EJ)]
        ein_loaded = [sem("ein_loaded0"), sem("ein_loaded1")]
        ein_turned, einT_copied = sem("ein_turned"), sem("einT_copied")
        hidden_summed, gelu_done = sem("hidden_summed"), sem("gelu_done")
        message_summed, gate_summed = sem("message_summed"), sem("gate_summed")
        tanh_done, gate_done, gated = sem("tanh_done"), sem("gate_done"), sem("gated")
        mask_loaded = [sem("mask_loaded0"), sem("mask_loaded1")]
        scanned, agg_summed, agg_copied = sem("scanned"), sem("agg_summed"), sem("agg_copied")
        agg_added = [sem(f"agg_added{j}") for j in range(EJ)]
        pre_loaded = [sem("pre_loaded0"), sem("pre_loaded1")]
        xn_loaded = [sem("xn_loaded0"), sem("xn_loaded1")]
        pre_turned, node_gelu, update_summed = sem("pre_turned"), sem("node_gelu"), sem("update_summed")
        h_made, xb_made, zg_made, y_made = sem("h_made"), sem("xb_made"), sem("zg_made"), sem("y_made")
        stats_step, root_step, norms_ready = sem("stats_step"), sem("root_step"), sem("norms_ready")
        h_measured, y_measured = sem("h_measured"), sem("y_measured")
        z_made, x1_made, out_made = sem("z_made"), sem("x1_made"), sem("out_made")
        x1_stored = [sem("x1_stored0"), sem("x1_stored1")]
        out_stored = [sem("out_stored0"), sem("out_stored1")]
        xd_gathered = [sem(f"xd_gathered{j}") for j in range(EJ)]
        x1s_gathered = [sem(f"x1s_gathered{j}") for j in range(EJ)]
        x1d_loaded = [sem("x1d_loaded0"), sem("x1d_loaded1")]
        ea_loaded = [sem("ea_loaded0"), sem("ea_loaded1")]
        cmask_loaded = [sem("cmask_loaded0"), sem("cmask_loaded1")]
        ops_turned, opsT_copied = sem("ops_turned"), sem("opsT_copied")
        k_summed, q_summed, e_summed, v_summed = (sem(n) for n in ("k_summed", "q_summed", "e_summed", "v_summed"))
        k_biased, kq_made, kqe_made = sem("k_biased"), sem("kq_made"), sem("kqe_made")
        heads_summed, clipped, score_made = sem("heads_summed"), sem("clipped"), sem("score_made")
        weighed, cscanned, seg_turned = sem("weighed"), sem("cscanned"), sem("seg_turned")
        z_step, hc_made, yc_made = sem("z_step"), sem("hc_made"), sem("yc_made")
        cstats_step, croot_step, cnorm_ready = sem("cstats_step"), sem("croot_step"), sem("cnorm_ready")
        fin_made = sem("fin_made")
        out_scattered = [sem(f"out_scattered{j}") for j in range(EJ)]

        columns = [(mb1s, mb1), (gb1s, gb1), (ub1s, ub1), (mb2s, mb2), (bqs, bq), (bks, bk), (bes, be)]
        WEIGHTS = 16 * (18 + len(columns))

        def slot_total(slot):
            return 16 * len(range(slot, NGROUPS, 2))

        def node_rows(t, g):
            at = min(g * NROWS, N - NROWS) if isinstance(g, int) else g * NROWS
            return t[bass.DynSlice(at, NROWS), :].rearrange("(p j) f -> p (j f)", j=NJ)

        block = ctx.enter_context(nc.Block())

        @block.sync
        def _(sp):
            for to, of in ((ident, ident_c), (heads, heads_c), (mW1s, mW1), (gW1s, gW1), (mW2s, mW2),
                           (gW2c, gW2), (uW1x, uW1[0:D, :]), (uW1a, uW1[D:2 * D, :]),
                           (Wqs, Wq), (Wks, Wk), (Wes, We)):
                sp.dma_start(to[:], of).then_inc(weights_loaded, 16)
            sp.dma_start(uW2s[0:D, :], uW2).then_inc(weights_loaded, 16)
            sp.dma_start(uW2s[D:D + 1, :], ub2.rearrange("(a d) -> a d", a=1)).then_inc(weights_loaded, 16)
            for to, of in columns:
                sp.dma_start(to[:], of.rearrange("(d a) -> d a", a=1)).then_inc(weights_loaded, 16)
            sp.dma_start(gb2s[:], gb2.rearrange("(d a) -> d a", a=1).broadcast_to([D, 1])).then_inc(weights_loaded, 16)
            for to, of in ((lng, ln_g), (lnb, ln_b)):
                sp.dma_start(to[:], of.rearrange("(a d) -> a d", a=1).broadcast_to([P, D])).then_inc(weights_loaded, 16)
            sp.wait_ge(pads_set, 6)
            sp.dma_start(Wvs[:, 0:D], Wv).then_inc(weights_loaded, 16)
            sp.dma_start(bvs[0:D, :], bv.rearrange("(d a) -> d a", a=1)).then_inc(weights_loaded, 16)
            sp.dma_start(spare[:], spare_c).then_inc(index_loaded, 16)
            for to, of in ((src_i, src), (dst_i, dst)):
                sp.dma_start(to[:, 0:EFULL, :], of[0:EFULL * EROWS].rearrange("(g p j) -> p g j", p=P, j=EJ)).then_inc(index_loaded, 16)
                sp.dma_start(to[0:ETAIL_P, EFULL, :], of[EFULL * EROWS:E].rearrange("(p j) -> p j", j=EJ)).then_inc(index_loaded, 16)
            sp.dma_start(next_i[:, 0:EFULL, :], dst[1:EFULL * EROWS + 1].rearrange("(g p j) -> p g j", p=P, j=EJ)).then_inc(index_loaded, 16)
            sp.dma_start(next_i[0:ETAIL_P - 1, EFULL, :], dst[EFULL * EROWS + 1:E - EJ + 1].rearrange("(p j) -> p j", j=EJ)).then_inc(index_loaded, 16)
            sp.dma_start(bounds[:], bounds_c).then_inc(index_loaded, 16)
            sp.dma_start(next_i[ETAIL_P - 1:ETAIL_P, EFULL, 0:EJ - 1], dst[E - EJ + 1:E].rearrange("(a j) -> a j", a=1)).then_inc(index_loaded, 16)
            sp.dma_start(pre_d[N:N + EROWS, :].rearrange("(p j) f -> p (j f)", j=EJ), zeros[:]).then_inc(spare_zeroed, 16)
            sp.wait_ge(same_made, 1)
            sp.dma_start(cont_d[:, 0:1], zeros[0:1, 0:1]).then_inc(cont_stored, 16)
            sp.dma_start(cont_d[:, 1:1 + EGROUPS * EROWS].rearrange("a (g p j) -> (a p) g j", p=P, j=EJ), same[:]).then_inc(cont_stored, 16)

            def node_step(i, s, inner):
                if inner or i + 1 < NGROUPS:
                    if inner or i >= 1:
                        sp.wait_ge(x_turned, i)
                    sp.dma_start(x_in[:, 1 - s, :], node_rows(x, i + 1)).then_inc(x_loaded[1 - s], 16)
                if inner or i >= 1:
                    sp.wait_ge(pre_copied, i)
                    if isinstance(i, int) and i == NGROUPS:
                        sp.wait_ge(pre_stored[s], slot_total(s))
                    sp.dma_start(node_rows(pre_d, i - 1), pre_io[:, 1 - s, :]).then_inc(pre_stored[1 - s], 16)

            sweep(sp, -1, NGROUPS + 1, 3, 3, node_step)

            def edge_step(i, s, inner):
                if inner or i + 1 < EGROUPS:
                    if inner or i >= 1:
                        sp.wait_ge(ein_turned, i)
                    for j in range(EJ):
                        sp.wait_ge(xs_gathered[j], i * 16 + 32)
                    sp.dma_start(ein[:, 1 - s, :, 0:D], rows[:, bass.DynSlice(i * EJ + EJ, EJ), :]).then_inc(ein_loaded[1 - s], 16)
                    if isinstance(i, int) and i + 1 == EFULL:
                        sp.dma_start(ein[0:ETAIL_P, 1 - s, :, D:D + DE], ea32[EFULL * EROWS:E, :].rearrange("(p j) f -> p j f", j=EJ)).then_inc(ein_loaded[1 - s], 16)
                    else:
                        sp.dma_start(ein[:, 1 - s, :, D:D + DE], ea32[bass.DynSlice(i * EROWS + EROWS, EROWS), :].rearrange("(p j) f -> p j f", j=EJ)).then_inc(ein_loaded[1 - s], 16)
                if inner or i + 1 < EGROUPS:
                    sp.wait_ge(cont_stored, 32)
                    if inner or i >= 1:
                        sp.wait_ge(scanned, i)
                    sp.dma_start(mask[0:D, 1 - s, :], cont_d[:, bass.DynSlice(i * EROWS + EROWS, EROWS)].broadcast_to([D, EROWS])).then_inc(mask_loaded[1 - s], 16)

            sweep(sp, -1, EGROUPS - 1, 3, 1, edge_step)

            sp.wait_ge(needs_made, 4)

            def update_step(i, s, inner):
                if inner or i + 2 < NGROUPS:
                    if inner or i >= 0:
                        sp.wait_ge(pre_turned, i + 1)
                    need = sp.value_load(need_agg[0:1, bass.DynSlice(i + 2, 1)], min_val=16, max_val=16 * EGROUPS)
                    for j in range(EJ):
                        sp.wait_ge(agg_added[j], need)
                    sp.wait_ge(pre_stored[s], slot_total(s))
                    sp.dma_start(pre_io[:, s, :], node_rows(pre_d, i + 2)).then_inc(pre_loaded[s], 16)
                if inner or -1 <= i < NGROUPS - 1:
                    if inner or i >= 1:
                        sp.wait_ge(xb_made, i)
                    sp.dma_start(x_in[:, 1 - s, :], node_rows(x, i + 1)).then_inc(xn_loaded[1 - s], 16)
                if inner or 5 <= i < NGROUPS + 5:
                    sp.wait_ge(x1_made, i - 4)
                    if isinstance(i, int) and i == NGROUPS + 4:
                        sp.wait_ge(x1_stored[s], slot_total(s))
                    sp.dma_start(node_rows(x1_d, i - 5), x1o[:, 1 - s, :]).then_inc(x1_stored[1 - s], 16)
                if inner or i >= 6:
                    sp.wait_ge(out_made, i - 5)
                    if isinstance(i, int) and i == NGROUPS + 5:
                        sp.wait_ge(out_stored[1 - s], slot_total(1 - s))
                    sp.dma_start(node_rows(out, i - 6), oo[:, s, :]).then_inc(out_stored[s], 16)

            sweep(sp, -2, NGROUPS + 6, 8, 9, update_step)

            def attend_step(i, s, inner):
                if inner or i + 1 < EGROUPS:
                    if inner or i >= 1:
                        sp.wait_ge(ops_turned, i * 3)
                    for j in range(EJ):
                        sp.wait_ge(xd_gathered[j], i * 16 + 32)
                    sp.dma_start(x1d[:, 1 - s, :, :], rows[:, bass.DynSlice(i * EJ + EJ, EJ), :]).then_inc(x1d_loaded[1 - s], 16)
                    if isinstance(i, int) and i + 1 == EFULL:
                        sp.dma_start(ea[0:ETAIL_P, 1 - s, :, :], ea96[EFULL * EROWS:E, :].rearrange("(p j) f -> p j f", j=EJ)).then_inc(ea_loaded[1 - s], 16)
                    else:
                        sp.dma_start(ea[:, 1 - s, :, :], ea96[bass.DynSlice(i * EROWS + EROWS, EROWS), :].rearrange("(p j) f -> p j f", j=EJ)).then_inc(ea_loaded[1 - s], 16)
                if inner or i + 1 < EGROUPS:
                    sp.wait_ge(cont_stored, 32)
                    if inner or i >= 1:
                        sp.wait_ge(cscanned, i)
                    sp.dma_start(mask[:, 1 - s, :], cont_d[:, bass.DynSlice(i * EROWS + EROWS, EROWS)].broadcast_to([DH, EROWS])).then_inc(cmask_loaded[1 - s], 16)

            sweep(sp, -1, EGROUPS - 1, 3, 1, attend_step)
            for j in range(EJ):
                sp.wait_ge(out_scattered[j], 16 * EGROUPS)

        @block.gpsimd
        def _(pool):
            def rows_at(index, g, j):
                return bass.IndirectOffsetOnAxis(ap=index[:, g, j:j + 1], axis=0)

            pool.wait_ge(index_loaded, 16 * 9)
            pool.wait_ge(index_made, 3)
            pool.wait_ge(needs_made, 4)
            for g in range(EGROUPS):
                for j in range(EJ):
                    if g >= 1:
                        pool.wait_ge(xs_gathered[j], 16 * g)
                    pool.indirect_dma_start(rows[:, g * EJ + j, :], None, x, rows_at(src_i, g, j)).then_inc(xs_gathered[j], 16)
            pool.wait_ge(spare_zeroed, 16)
            for s in range(2):
                pool.wait_ge(pre_stored[s], slot_total(s))
            for g in range(EGROUPS):
                pool.wait_ge(agg_copied, g + 1)
                for j in range(EJ):
                    if g >= 1:
                        pool.wait_ge(agg_added[j], 16 * g)
                    pool.indirect_dma_start(pre_d, rows_at(add_at, g, j), rows[:, g * EJ + j, :], None,
                                            bounds_check=N + EROWS - 1, oob_is_err=True,
                                            compute_op=ALU.add).then_inc(agg_added[j], 16)
            for g in range(EGROUPS):
                needs = [pool.value_load(need_x1[0:1, s, g:g + 1], min_val=16, max_val=slot_total(0)) for s in range(2)]
                for j in range(EJ):
                    if g == 0:
                        pool.wait_ge(agg_added[j], 16 * EGROUPS)
                    else:
                        pool.wait_ge(xd_gathered[j], 16 * g)
                for s in range(2):
                    pool.wait_ge(x1_stored[s], needs[s])
                for j in range(EJ):
                    pool.indirect_dma_start(rows[:, g * EJ + j, :], None, x1_d, rows_at(dst_at, g, j)).then_inc(xd_gathered[j], 16)
            for s in range(2):
                pool.wait_ge(x1_stored[s], slot_total(s))
            LAG = 5
            for g in range(EGROUPS + LAG):
                if g < EGROUPS:
                    if g >= 2:
                        pool.wait_ge(ops_turned, 3 * (g - 1))
                    for j in range(EJ):
                        if g >= 1:
                            pool.wait_ge(x1s_gathered[j], 16 * g)
                        pool.indirect_dma_start(x1s[:, g % 2, j, :], None, x1_d, rows_at(src_i, g, j)).then_inc(x1s_gathered[j], 16)
                b = g - LAG
                if b == 0:
                    for s in range(2):
                        pool.wait_ge(out_stored[s], slot_total(s))
                if b >= 0:
                    pool.wait_ge(fin_made, b + 1)
                    for j in range(EJ):
                        if b >= 1:
                            pool.wait_ge(out_scattered[j], 16 * b)
                        pool.indirect_dma_start(out, rows_at(put_at, b, j), fin[:, b % 2, j, :], None,
                                                bounds_check=N - 1, oob_is_err=False).then_inc(out_scattered[j], 16)

        @block.tensor
        def _(pe):
            pe.wait_ge(weights_loaded, WEIGHTS)
            pe.wait_ge(weights_made, 3)

            def turn(to, of, last=None):
                mmx = pe.transpose(to, of, ident[:, :])
                if last is not None:
                    mmx.then_inc(last, 1)

            def node_step(i, s, inner):
                if inner or i < NGROUPS:
                    pe.wait_ge(x_loaded[s], per_slot(i, s))
                    if inner or i >= 2:
                        pe.wait_ge(xT_copied, i - 1)
                    for j in range(NJ):
                        turn(ps[0:D, 2 * s + j // 4, (j % 4) * P:(j % 4 + 1) * P], x_in[:, s, j * D:(j + 1) * D],
                             x_turned if j == NJ - 1 else None)
                if inner or i >= 1:
                    pe.wait_ge(xT_copied, i)
                    if inner or i >= 3:
                        pe.wait_ge(pre_copied, i - 2)
                    for j in range(NJ):
                        m = pe.matmul(ps[:, 4 + 2 * (1 - s) + j // 4, (j % 4) * D:(j % 4 + 1) * D],
                                      nT[0:D, 1 - s, j * P:(j + 1) * P], uW1x[:, :], start=True, stop=True)
                    m.then_inc(pre_summed, 1)

            sweep(pe, 0, NGROUPS + 1, 3, 1, node_step)

            pe.wait_ge(xT_copied, NGROUPS)
            pe.wait_ge(pre_copied, NGROUPS)

            def edge_step(i, s, inner):
                if inner or 0 <= i < EGROUPS:
                    pe.wait_ge(einT_copied, i + 1)
                    if inner or i >= 1:
                        pe.wait_ge(gelu_done, i * 2)
                    pe.matmul(ps[0:D, 2, :], mW1s[:, :], einT[:, s, :], start=True, stop=True).then_inc(hidden_summed, 1)
                    pe.matmul(ps[0:D, 3, :], gW1s[:, :], einT[:, s, :], start=True, stop=True).then_inc(hidden_summed, 1)
                if inner or i + 1 < EGROUPS:
                    pe.wait_ge(ein_loaded[1 - s], (i + 1) * 16 + (32 - 16 * (1 - s)))
                    if inner or i >= 1:
                        pe.wait_ge(einT_copied, i)
                    to = ps[:, 1 - s, :].rearrange("p (c j) -> p j c", j=EJ)
                    for j in range(EJ):
                        turn(to[:, j, :], ein[:, 1 - s, j, :], ein_turned if j == EJ - 1 else None)
                if inner or 0 <= i < EGROUPS:
                    pe.wait_ge(gelu_done, i * 2 + 1)
                    if inner or i >= 1:
                        pe.wait_ge(gated, i)
                    pe.matmul(ps[0:D, 4, :], mW2s[:, :], gm[:, :], start=True, stop=True).then_inc(message_summed, 1)
                    pe.wait_ge(gelu_done, i * 2 + 2)
                    if inner or i >= 1:
                        pe.wait_ge(tanh_done, i)
                    pe.matmul(ps[0:D, 5, :], gW2s[:, :], gg[:, :], start=True, stop=True).then_inc(gate_summed, 1)
                if inner or i >= 1:
                    pe.wait_ge(scanned, i)
                    if inner or i >= 3:
                        pe.wait_ge(agg_copied, i - 2)
                    of = seg[0:D, 1 - s, :].rearrange("p (c j) -> p j c", j=EJ)
                    for j in range(EJ):
                        m = pe.matmul(ps[:, 6 + (1 - s), j * D:(j + 1) * D], of[:, j, :], uW1a[:, :], start=True, stop=True)
                    m.then_inc(agg_summed, 1)

            sweep(pe, -1, EGROUPS + 1, 4, 2, edge_step)

            pe.wait_ge(einT_copied, EGROUPS)
            pe.wait_ge(gelu_done, 2 * EGROUPS)
            pe.wait_ge(gated, EGROUPS)
            pe.wait_ge(tanh_done, EGROUPS)
            pe.wait_ge(agg_copied, EGROUPS)

            def update_step(i, s, inner):
                if inner or i >= 0:
                    pe.wait_ge(node_gelu, i + 1)
                    if inner or i >= 2:
                        pe.wait_ge(h_made, i - 1)
                    for j in range(NJ):
                        m = pe.matmul(ps[:, 4 + 2 * s + j // 4, (j % 4) * D:(j % 4 + 1) * D],
                                      nT[:, s, j * P:(j + 1) * P], uW2s[:, :], start=True, stop=True)
                    m.then_inc(update_summed, 1)
                if inner or i + 1 < NGROUPS:
                    pe.wait_ge(pre_loaded[1 - s], per_slot(i + 1, 1 - s))
                    if inner or i >= 1:
                        pe.wait_ge(node_gelu, i)
                    for j in range(NJ):
                        turn(ps[0:D, 2 * (1 - s) + j // 4, (j % 4) * P:(j % 4 + 1) * P], pre_io[:, 1 - s, j * D:(j + 1) * D],
                             pre_turned if j == NJ - 1 else None)

            sweep(pe, -1, NGROUPS, 3, 1, update_step)

            pe.wait_ge(node_gelu, NGROUPS)
            pe.wait_ge(h_made, NGROUPS)

            def attend_step(i, s, inner):
                if inner or 0 <= i < EGROUPS:
                    pe.wait_ge(opsT_copied, i * 3 + 3)
                    xsT, xdT, eaT = opT[s]
                    if inner or i >= 1:
                        pe.wait_ge(k_biased, i)
                    pe.matmul(ps[0:D, 3, :], Wks[:, :], xsT, start=True, stop=True).then_inc(k_summed, 1)
                    if inner or i >= 1:
                        pe.wait_ge(kq_made, i)
                    pe.matmul(ps[0:D, 4, :], Wqs[:, :], xdT, start=True, stop=True).then_inc(q_summed, 1)
                    if inner or i >= 1:
                        pe.wait_ge(clipped, i)
                    pe.matmul(ps[0:D, 5, :], Wes[:, :], eaT, start=True, stop=True).then_inc(e_summed, 1)
                    if inner or i >= 1:
                        pe.wait_ge(weighed, i)
                    pe.matmul(ps[0:DH, 6, :], Wvs[:, :], xsT, start=True, stop=True).then_inc(v_summed, 1)
                if inner or i >= 1:
                    pe.wait_ge(cscanned, i)
                    if inner or i >= 2:
                        pe.wait_ge(hc_made, i - 1)
                    of = seg[:, 1 - s, :].rearrange("p (c j) -> p j c", j=EJ)
                    for j in range(EJ):
                        m = pe.transpose(ps[:, 7, j * DH:(j + 1) * DH], of[:, j, :], ident[0:DH, 0:DH])
                    m.then_inc(seg_turned, 1)
                if inner or i + 1 < EGROUPS:
                    for j in range(EJ):
                        pe.wait_ge(x1s_gathered[j], i * 16 + 32)
                    pe.wait_ge(x1d_loaded[1 - s], per_slot(i + 1, 1 - s))
                    pe.wait_ge(ea_loaded[1 - s], per_slot(i + 1, 1 - s))
                    if inner or i >= 0:
                        pe.wait_ge(opsT_copied, i * 3 + 3)
                    for b, of in enumerate((x1s, x1d, ea)):
                        to = ps[0:D, b, :].rearrange("p (c j) -> p j c", j=EJ)
                        for j in range(EJ):
                            turn(to[:, j, :], of[:, 1 - s, j, :], ops_turned if j == EJ - 1 else None)
                if inner or 0 <= i < EGROUPS:
                    pe.wait_ge(kqe_made, i + 1)
                    pe.matmul(ps[0:DH, 5, :], heads[:, :], kqe[:, :], start=True, stop=True).then_inc(heads_summed, 1)

            sweep(pe, -1, EGROUPS + 1, 4, 2, attend_step)

        @block.scalar
        def _(act):
            act.wait_ge(weights_loaded, WEIGHTS)
            act.wait_ge(weights_made, 5)

            def node_step(i, s, inner):
                act.wait_ge(x_turned, i + 1)
                if inner or i >= 2:
                    act.wait_ge(pre_summed, i - 1)
                act.activation(nT[0:D, s, :].rearrange("p (b c) -> p b c", b=2), ps[0:D, 2 * s:2 * s + 2, :], ACT.Copy).then_inc(xT_copied, 1)

            sweep(act, 0, NGROUPS, 3, 0, node_step)

            def edge_step(i, s, inner):
                if inner or i >= 0:
                    act.wait_ge(hidden_summed, i * 2 + 1)
                    if inner or i >= 1:
                        act.wait_ge(message_summed, i)
                    act.activation(gm[:, :], ps[0:D, 2, :], ACT.Gelu, bias=mb1s[:, 0:1]).then_inc(gelu_done, 1)
                    act.wait_ge(hidden_summed, i * 2 + 2)
                    if inner or i >= 1:
                        act.wait_ge(gate_summed, i)
                    act.activation(gg[:, :], ps[0:D, 3, :], ACT.Gelu, bias=gb1s[:, 0:1]).then_inc(gelu_done, 1)
                if inner or i + 1 < EGROUPS:
                    act.wait_ge(ein_turned, i + 2)
                    if inner or i >= 1:
                        act.wait_ge(hidden_summed, i * 2)
                    act.activation(einT[:, 1 - s, :], ps[:, 1 - s, :], ACT.Copy).then_inc(einT_copied, 1)
                if inner or i >= 0:
                    act.wait_ge(gate_summed, i + 1)
                    if inner or i >= 1:
                        act.wait_ge(gated, i)
                    act.activation(gate[:, :], ps[0:D, 5, :], ACT.Tanh, bias=gb2s[:, 0:1], scale=0.5).then_inc(tanh_done, 1)

            sweep(act, -1, EGROUPS, 4, 1, edge_step)

            def update_step(i, s, inner):
                k = 1 - s
                if inner or i >= 2:
                    act.wait_ge(norms_ready, i)
                if inner or 2 <= i < NGROUPS + 2:
                    if inner or i >= 4:
                        act.wait_ge(zg_made, i - 3)
                        act.wait_ge(y_made, i - 3)
                    for j in range(NJ):
                        o = act.activation(z[:, s, j * D:(j + 1) * D], h[:, s, j * D:(j + 1) * D], ACT.Identity,
                                           bias=nshift[:, k, 0, j:j + 1], scale=nscale[:, k, 0, j:j + 1])
                    o.then_inc(z_made, 1)
                if inner or i + 1 < NGROUPS:
                    act.wait_ge(pre_turned, i + 2)
                    if inner or i >= 1:
                        act.wait_ge(update_summed, i)
                    act.activation(nT[0:D, 1 - s, :].rearrange("p (b c) -> p b c", b=2), ps[0:D, 2 * (1 - s):2 * (1 - s) + 2, :], ACT.Gelu, bias=ub1s[:, 0:1]).then_inc(node_gelu, 1)
                if inner or 4 <= i < NGROUPS + 4:
                    if inner or i >= 6:
                        act.wait_ge(x1_stored[s], per_slot(i - 6, s))
                        act.wait_ge(out_made, i - 5)
                    for j in range(NJ):
                        o = act.activation(x1o[:, s, j * D:(j + 1) * D], y[:, s, j * D:(j + 1) * D], ACT.Identity,
                                           bias=nshift[:, k, 1, j:j + 1], scale=nscale[:, k, 1, j:j + 1])
                    o.then_inc(x1_made, 1)
                if inner or i >= 5:
                    if inner or i >= 7:
                        act.wait_ge(out_stored[1 - s], per_slot(i - 7, 1 - s))
                    act.wait_ge(x1_made, i - 4)
                    for j in range(NJ):
                        o = act.activation(oo[:, 1 - s, j * D:(j + 1) * D], x1o[:, 1 - s, j * D:(j + 1) * D], ACT.Identity,
                                           scale=nscale[:, k, 2, j:j + 1])
                    o.then_inc(out_made, 1)

            sweep(act, -1, NGROUPS + 5, 8, 6, update_step)

            def attend_step(i, s, inner):
                if inner or 0 <= i < EGROUPS:
                    act.wait_ge(k_summed, i + 1)
                    if inner or i >= 1:
                        act.wait_ge(kq_made, i)
                    act.activation(kS[:, :], ps[0:D, 3, :], ACT.Identity, bias=bks[:, 0:1]).then_inc(k_biased, 1)
                if inner or i >= 3:
                    act.wait_ge(cnorm_ready, i - 2)
                    if inner or i >= 5:
                        for j in range(EJ):
                            act.wait_ge(out_scattered[j], i * 16 - 64)
                    for j in range(EJ):
                        o = act.activation(fin[:, 1 - s, j, :], yc[:, 1 - s, j, :], ACT.Identity,
                                           bias=cshift[:, 1 - s, j:j + 1], scale=cscale[:, 1 - s, j:j + 1])
                    o.then_inc(fin_made, 1)
                if inner or i + 1 < EGROUPS:
                    for b in range(3):
                        act.wait_ge(ops_turned, i * 3 + 4 + b)
                        if b == 0 and (inner or i >= 1):
                            act.wait_ge(v_summed, i)
                            act.wait_ge(e_summed, i)
                            act.wait_ge(q_summed, i)
                        act.activation(opT[1 - s][b], ps[0:D, b, :], ACT.Copy).then_inc(opsT_copied, 1)
                if inner or 0 <= i < EGROUPS:
                    act.wait_ge(clipped, i + 1)
                    if inner or i >= 1:
                        act.wait_ge(weighed, i)
                    act.activation(score[:, :], clip[:, :], ACT.Exp).then_inc(score_made, 1)

            sweep(act, -1, EGROUPS + 3, 7, 4, attend_step)

        @block.vector
        def _(dve):
            dve.memset(src_i[:, EFULL, :], 0).then_inc(pads_set, 1)
            dve.memset(dst_i[:, EFULL, :], FAR).then_inc(pads_set, 1)
            dve.memset(next_i[:, EFULL, :], FAR).then_inc(pads_set, 1)
            dve.memset(zeros[:, :], 0.0).then_inc(pads_set, 1)
            dve.memset(Wvs[:, :], 0.0).then_inc(pads_set, 1)
            dve.memset(bvs[:, :], 1.0).then_inc(pads_set, 1)
            dve.memset(nT[D:D + 1, :, :], 1.0).then_inc(weights_made, 1)
            dve.wait_ge(index_loaded, 16 * 9)
            dve.tensor_tensor(same[:, :, :], dst_i[:, :, :], next_i[:, :, :], ALU.is_equal).then_inc(same_made, 1)
            dve.tensor_tensor(shift[:, :, :], spare[:, :].unsqueeze(1).broadcast_to([P, EGROUPS, EJ]), dst_i[:, :, :], ALU.subtract).then_inc(same_made, 1)
            dve.tensor_scalar(dst_at[:, :, :], dst_i[:, :, :], N - 1, None, ALU.min).then_inc(index_made, 1)
            dve.wait_ge(same_made, 2)
            dve.tensor_tensor(shift[:, :, :], shift[:, :, :], same[:, :, :], ALU.mult).then_inc(same_made, 1)
            dve.scalar_tensor_tensor(put_at[:, :, :], same[:, :, :], float(FAR), dst_i[:, :, :], ALU.mult, ALU.add).then_inc(index_made, 1)
            dve.wait_ge(same_made, 3)
            dve.tensor_tensor(add_at[:, :, :], dst_i[:, :, :], shift[:, :, :], ALU.add).then_inc(index_made, 1)
            dve.memset(group_dst[:, EGROUPS:], FAR).then_inc(needs_step, 1)
            dve.tensor_copy(group_dst[:, 0:EGROUPS], dst_i[0:1, :, 0]).then_inc(needs_step, 1)
            dve.wait_ge(needs_step, 2)

            def count_pairs(k, of, other, op):
                dve.tensor_tensor(below[:, :, :], of, other, op).then_inc(needs_step, 1)
                dve.wait_ge(needs_step, 2 * k + 3)
                dve.tensor_reduce(counts[:, k, :], below[:, :, :], mybir.AxisListType.X, ALU.add).then_inc(needs_step, 1)
                dve.wait_ge(needs_step, 2 * k + 4)

            wide = [1, EGROUPS, NGROUPS]
            count_pairs(0, group_dst[:, 0:EGROUPS].unsqueeze(1).broadcast_to(wide), bounds[:, 0, :].unsqueeze(2).broadcast_to(wide), ALU.is_lt)
            count_pairs(1, bounds[:, 1, :].unsqueeze(1).broadcast_to(wide), group_dst[:, 1:].unsqueeze(2).broadcast_to(wide), ALU.is_le)
            dve.tensor_scalar(need_agg[:, :], counts[:, 0, :], 1.0, 16.0, ALU.max, ALU.mult).then_inc(needs_made, 1)
            dve.tensor_scalar(pairs[:, 0, :], counts[:, 1, :], 2.0, 1.0, ALU.max, ALU.add).then_inc(needs_step, 1)
            dve.tensor_scalar(pairs[:, 1, :], counts[:, 1, :], 2.0, None, ALU.max).then_inc(needs_step, 1)
            dve.wait_ge(needs_step, 8)
            dve.tensor_scalar(pairs[:, :, :], pairs[:, :, :], 1, None, ALU.arith_shift_right).then_inc(needs_made, 1)
            dve.wait_ge(needs_made, 2)
            dve.tensor_scalar(need_x1[:, :, :], pairs[:, :, :], 16, None, ALU.mult).then_inc(needs_made, 2)
            dve.wait_ge(pads_set, 6)
            dve.wait_ge(weights_loaded, WEIGHTS)
            dve.tensor_scalar(gW2s[:, :], zeros[0:D, 0:D], gW2c[:, 0:1], None, ALU.add).then_inc(weights_made, 1)
            dve.tensor_scalar(mW2s[:, :], mW2s[:, :], 0.5, None, ALU.mult).then_inc(weights_made, 1)
            dve.tensor_scalar(mb2s[:, :], mb2s[:, :], 0.5, None, ALU.mult).then_inc(weights_made, 1)
            dve.tensor_scalar(gb2s[:, :], gb2s[:, :], 0.5, None, ALU.mult).then_inc(weights_made, 1)

            def node_step(i, s, inner):
                dve.wait_ge(pre_summed, i + 1)
                if inner or i >= 2:
                    dve.wait_ge(pre_stored[s], per_slot(i - 2, s))
                dve.tensor_copy(pre_io[:, s, :].rearrange("p (b c) -> p b c", b=2), two_banks(4 + 2 * s)).then_inc(pre_copied, 1)

            sweep(dve, 0, NGROUPS, 3, 0, node_step)
            dve.wait_ge(weights_made, 5)

            def edge_step(i, s, inner):
                if inner or i < EGROUPS:
                    dve.wait_ge(tanh_done, i + 1)
                    dve.tensor_scalar(gate[:, :], gate[:, :], 1.0, None, ALU.add).then_inc(gate_done, 1)
                    dve.wait_ge(gate_done, i + 1)
                    dve.wait_ge(message_summed, i + 1)
                    dve.scalar_tensor_tensor(mm[:, :], ps[0:D, 4, :], mb2s[:, 0:1], gate[:, :], ALU.add, ALU.mult).then_inc(gated, 1)
                    dve.wait_ge(gated, i + 1)
                    dve.wait_ge(mask_loaded[s], per_slot(i, s))
                    if inner or i >= 2:
                        dve.wait_ge(agg_summed, i - 1)
                    if inner or i >= 1:
                        dve.wait_ge(scanned, i)
                    before = seg[0:D, 1 - s, EROWS - 1:EROWS] if inner or i >= 1 else 0.0
                    dve.tensor_tensor_scan(seg[0:D, s, :], mask[0:D, s, :], mm[:, :], before, ALU.mult, ALU.add).then_inc(scanned, 1)
                if inner or i >= 1:
                    dve.wait_ge(agg_summed, i)
                    dve.tensor_copy(rows[:, bass.DynSlice(i * EJ - EJ, EJ), :],
                                    ps[:, 6 + (1 - s), 0:EJ * D].rearrange("p (j f) -> p j f", j=EJ)).then_inc(agg_copied, 1)

            sweep(dve, 0, EGROUPS + 1, 3, 1, edge_step)

            lngb = lng[:, :].unsqueeze(1).broadcast_to([P, NJ, D])
            lnbb = lnb[:, :].unsqueeze(1).broadcast_to([P, NJ, D])

            def rows_of(t, s):
                return t[:, s, :].rearrange("p (j f) -> p j f", j=NJ)

            def norm_op(k, stats, total, apart, squares, var, with_eps, guess, half, done, base):
                gi, vi = guess.bitcast(I32), with_eps.bitcast(I32)
                if k == 3:
                    dve.wait_ge(done, base + 2)
                elif k > 3:
                    dve.wait_ge(done, base + k)
                if k == 0:
                    ins = dve.tensor_tensor(total, stats(1), stats(4), ALU.add)
                elif k == 1:
                    ins = dve.tensor_tensor(apart, stats(1), stats(4), ALU.subtract)
                elif k == 2:
                    ins = dve.tensor_tensor(squares, stats(2), stats(5), ALU.add)
                elif k == 3:
                    ins = dve.scalar_tensor_tensor(apart, apart, 0.25, apart, ALU.mult, ALU.mult)
                elif k == 4:
                    ins = dve.scalar_tensor_tensor(var[0], squares, 1.0 / D, apart, ALU.mult, ALU.add)
                elif k == 5:
                    ins = dve.tensor_scalar(with_eps, var[1], EPS, None, ALU.add)
                elif k == 6:
                    ins = dve.tensor_scalar(gi, vi, 1, None, ALU.arith_shift_right)
                elif k == 7:
                    ins = dve.tensor_scalar(gi, gi, -1, MAGIC, ALU.mult, ALU.add)
                elif k % 3 == 2:
                    ins = dve.scalar_tensor_tensor(half, guess, -0.5, guess, ALU.mult, ALU.mult)
                elif k % 3 == 0:
                    ins = dve.tensor_tensor(half, half, with_eps, ALU.mult)
                else:
                    ins = dve.scalar_tensor_tensor(guess, half, 1.5, guess, ALU.add, ALU.mult)
                ins.then_inc(done, 1)

            dve.memset(bn[:, :, :, :], 1.0).then_inc(stats_step, 1)
            dve.memset(nv[:, :, :], 1.0).then_inc(stats_step, 1)
            dve.wait_ge(stats_step, 2)
            flat = lambda t: t[:, :, :].rearrange("p a j -> p (a j)")
            NSTEPS = 17 + 3

            def update_step(i, s, inner):
                def norm(k):
                    norm_op(k, lambda m: bn[:, :, :, m], msum[:, :, :], mdif[:, :, :], sqs[:, :, :],
                            (nv[:, 0:2, :], nv[:, :, :]), nvar[:, :, :], nroot[:, :, :], nhalf[:, :, :],
                            root_step, i * NSTEPS)

                if inner or 1 <= i < NGROUPS + 1:
                    dve.wait_ge(h_measured, i)
                if inner or 3 <= i < NGROUPS + 3:
                    dve.wait_ge(y_measured, i - 2)
                for k in range(3):
                    norm(k)
                if inner or i < NGROUPS:
                    dve.wait_ge(update_summed, i + 1)
                    dve.wait_ge(xn_loaded[s], per_slot(i, s))
                    if inner or i >= 2:
                        dve.wait_ge(z_made, i - 1)
                    dve.tensor_tensor(h[:, s, :].rearrange("p (b c) -> p b c", b=2), two_banks(4 + 2 * s),
                                      x_in[:, s, :].rearrange("p (b c) -> p b c", b=2), ALU.add).then_inc(h_made, 1)
                    norm(3)
                    dve.wait_ge(h_made, i + 1)
                    for j in range(NJ):
                        b = dve.bn_stats(bn[:, 0, j, :], h[:, s, j * D:(j + 1) * D])
                        if j == NJ - 1:
                            b.then_inc(h_measured, 1)
                        if j < 5:
                            norm(4 + j)
                else:
                    for k in range(3, 9):
                        norm(k)
                if inner or 2 <= i < NGROUPS + 2:
                    dve.wait_ge(z_made, i - 1)
                    dve.tensor_tensor(rows_of(z, s), rows_of(z, s), lngb, ALU.mult).then_inc(zg_made, 1)
                    norm(9)
                    if inner or i >= 4:
                        dve.wait_ge(x1_made, i - 3)
                    dve.wait_ge(zg_made, i - 1)
                    dve.tensor_tensor(y[:, s, :], z[:, s, :], xb[:, s, :], ALU.add).then_inc(y_made, 1)
                else:
                    norm(9)
                norm(10)
                norm(11)
                if inner or 2 <= i < NGROUPS + 2:
                    dve.wait_ge(y_made, i - 1)
                    for j in range(NJ):
                        b = dve.bn_stats(bn[:, 1, j, :], y[:, s, j * D:(j + 1) * D])
                        if j == NJ - 1:
                            b.then_inc(y_measured, 1)
                        if j < 5:
                            norm(12 + j)
                else:
                    for k in range(12, 17):
                        norm(k)
                if inner or i < NGROUPS:
                    dve.tensor_tensor(rows_of(xb, s), rows_of(x_in, s), lnbb, ALU.add).then_inc(xb_made, 1)
                if inner or 3 <= i < NGROUPS + 3:
                    dve.wait_ge(z_made, i - 2)
                if inner or i >= 5:
                    dve.wait_ge(x1_made, i - 4)
                if inner or i >= 6:
                    dve.wait_ge(out_made, i - 5)
                dve.wait_ge(root_step, i * NSTEPS + 17)
                dve.scalar_tensor_tensor(nshift[:, s, :, :], msum[:, :, :], -0.5, nroot[:, 0:2, :], ALU.mult, ALU.mult).then_inc(root_step, 1)
                dve.tensor_tensor(nv[:, 2, :], nv[:, 1, :], nroot[:, 1, :], ALU.mult).then_inc(root_step, 1)
                dve.wait_ge(root_step, i * NSTEPS + 18)
                dve.tensor_copy(nscale[:, s, :, :], nroot[:, :, :]).then_inc(norms_ready, 1)
                dve.wait_ge(root_step, i * NSTEPS + 19)
                dve.tensor_tensor(nv[:, 2, :], nv[:, 2, :], nroot[:, 1, :], ALU.mult).then_inc(root_step, 1)
                dve.wait_ge(root_step, i * NSTEPS + 20)

            sweep(dve, 0, NGROUPS + 4, 7, 5, update_step)

            def attend_step(i, s, inner):
                def norm(k):
                    if inner or 2 <= i < EGROUPS + 2:
                        norm_op(k, lambda m: cbn[:, :, m], csum[:, :], cdif[:, :], csqs[:, :],
                                (cv[:, :], cv[:, :]), cvar[:, :], croot[:, :], chalf[:, :], croot_step, i * 18 - 36)

                if inner or i >= 2:
                    dve.wait_ge(cstats_step, i - 1)
                if inner or i >= 3:
                    dve.wait_ge(cnorm_ready, i - 2)
                for k in range(3):
                    norm(k)
                if inner or i < EGROUPS:
                    dve.wait_ge(q_summed, i + 1)
                    dve.wait_ge(k_biased, i + 1)
                    dve.scalar_tensor_tensor(kq[:, :], ps[0:D, 4, :], bqs[:, 0:1], kS[:, :], ALU.add, ALU.mult).then_inc(kq_made, 1)
                norm(3)
                if inner or i < EGROUPS:
                    dve.wait_ge(e_summed, i + 1)
                    dve.wait_ge(kq_made, i + 1)
                    if inner or i >= 1:
                        dve.wait_ge(heads_summed, i)
                    dve.scalar_tensor_tensor(kqe[:, :], ps[0:D, 5, :], bes[:, 0:1], kq[:, :], ALU.add, ALU.mult).then_inc(kqe_made, 1)
                norm(4)
                if inner or 1 <= i < EGROUPS + 1:
                    dve.wait_ge(seg_turned, i)
                    back = ps[:, 7, 0:EJ * DH].rearrange("p (j f) -> p j f", j=EJ)
                    dve.tensor_scalar(zr[:, 0, :, :], back[:, :, D:DH], 1e-6, None, ALU.add).then_inc(z_step, 1)
                    norm(5)
                    dve.wait_ge(z_step, i * 2 - 1)
                    dve.reciprocal(zr[:, 1, :, :], zr[:, 0, :, :]).then_inc(z_step, 1)
                    norm(6)
                    dve.wait_ge(z_step, i * 2)
                    for j in range(EJ):
                        b = dve.tensor_tensor(hc[:, j, :].rearrange("p (a d) -> p a d", a=HEADS),
                                              back[:, j, 0:D].rearrange("p (a d) -> p a d", a=HEADS),
                                              zr[:, 1, j, :].unsqueeze(2).broadcast_to([P, HEADS, HD]), ALU.mult)
                        if j == EJ - 1:
                            b.then_inc(hc_made, 1)
                        if j == 1:
                            norm(7)
                else:
                    for k in range(5, 8):
                        norm(k)
                norm(8)
                if inner or i < EGROUPS:
                    dve.wait_ge(heads_summed, i + 1)
                    if inner or i >= 1:
                        dve.wait_ge(score_made, i)
                    dve.tensor_scalar(clip[:, :], ps[0:DH, 5, :], -5.0, 5.0, ALU.max, ALU.min).then_inc(clipped, 1)
                norm(9)
                if inner or 1 <= i < EGROUPS + 1:
                    dve.wait_ge(hc_made, i)
                    if inner or i >= 3:
                        dve.wait_ge(fin_made, i - 2)
                    dve.tensor_tensor(yc[:, 1 - s, :, :], hc[:, :, :], rows[:, bass.DynSlice(i * EJ - EJ, EJ), :], ALU.add).then_inc(yc_made, 1)
                    norm(10)
                    dve.wait_ge(yc_made, i)
                    for j in range(EJ):
                        b = dve.bn_stats(cbn[:, j, :], yc[:, 1 - s, j, :])
                        if j == EJ - 1:
                            b.then_inc(cstats_step, 1)
                        else:
                            norm(11 + j)
                else:
                    for k in range(10, 14):
                        norm(k)
                if inner or i < EGROUPS:
                    dve.wait_ge(score_made, i + 1)
                    dve.wait_ge(v_summed, i + 1)
                    dve.scalar_tensor_tensor(msg[:, :], ps[0:DH, 6, :], bvs[:, 0:1], score[:, :], ALU.add, ALU.mult).then_inc(weighed, 1)
                norm(14)
                if inner or i < EGROUPS:
                    dve.wait_ge(weighed, i + 1)
                    dve.wait_ge(cmask_loaded[s], per_slot(i, s))
                    if inner or i >= 2:
                        dve.wait_ge(seg_turned, i - 1)
                    if inner or i >= 1:
                        dve.wait_ge(cscanned, i)
                    before = seg[:, 1 - s, EROWS - 1:EROWS] if inner or i >= 1 else 0.0
                    dve.tensor_tensor_scan(seg[:, s, :], mask[:, s, :], msg[:, :], before, ALU.mult, ALU.add).then_inc(cscanned, 1)
                norm(15)
                norm(16)
                if inner or i >= 2:
                    if inner or i >= 4:
                        dve.wait_ge(fin_made, i - 3)
                    dve.wait_ge(croot_step, i * 18 - 36 + 17)
                    dve.tensor_copy(cscale[:, s, :], croot[:, :]).then_inc(croot_step, 1)
                    dve.wait_ge(croot_step, i * 18 - 18)
                    dve.scalar_tensor_tensor(cshift[:, s, :], csum[:, :], -0.5, croot[:, :], ALU.mult, ALU.mult).then_inc(cnorm_ready, 1)

            sweep(dve, 0, EGROUPS + 2, 5, 3, attend_step)


_RENAMED = {"edge_attr_32": "ea32", "edge_attr_96": "ea96"}
_ORDER = ["x", "src", "dst", "edge_attr_32", "edge_attr_96"] + [
    f"L0_gnn_{n}" for n in ("mW1", "mb1", "mW2", "mb2", "gW1", "gb1", "gW2", "gb2", "uW1", "ub1", "uW2", "ub2", "ln_g", "ln_b")] + [
    f"L1_gnn_{n}" for n in ("Wq", "bq", "Wk", "bk", "We", "be", "Wv", "bv")]


def shape_constants():
    heads = np.zeros((D, DH), np.float32)
    for f in range(D):
        heads[f, f // HD * HD:(f // HD + 1) * HD] = HD ** -0.5
        heads[f, D + f // HD] = HD ** -0.5
    spare = (N + np.arange(P)[:, None] + P * np.arange(EJ)[None, :]).astype(np.int32)
    starts = np.minimum(np.arange(NGROUPS) * NROWS, N - NROWS)
    bounds = np.stack([starts + NROWS, starts])[None].astype(np.int32)
    return {"ident_c": np.eye(P, dtype=np.float32), "heads_c": heads, "spare_c": spare, "bounds_c": bounds}


def kernel(**inputs):
    import concourse.bacc as bacc
    from concourse.bass_utils import run_bass_kernel_spmd

    nc = bacc.Bacc("TRN2", target_bir_lowering=False, num_devices=1)
    arrays = {f"in_{n}": np.ascontiguousarray(inputs[n]) for n in _ORDER} | shape_constants()
    args = [nc.dram_tensor(n, a.shape, mybir.dt.from_np(a.dtype), kind="ExternalInput").ap() for n, a in arrays.items()]
    out = nc.dram_tensor("out", [N, D], F32, kind="ExternalOutput").ap()
    build(nc, *args, out)
    return run_bass_kernel_spmd(nc, [arrays], core_ids=[0]).results[0]["out"]
```

```python
from contextlib import ExitStack

import numpy as np

import concourse.bass as bass
from concourse import mybir

P = 128
N, E, D, DE = 50000, 25000, 96, 32
HEADS = 8
HD = D // HEADS
DH = D + HEADS
EJ = 4
EROWS = P * EJ
EGROUPS = -(-E // EROWS)
EFULL = EGROUPS - 1
ETAIL_P = (E - EFULL * EROWS) // EJ
NJ = 8
NROWS = P * NJ
NGROUPS = -(-N // NROWS)
ZJ = 10
ZSTEPS = -(-(N + 2 * EROWS) // (P * ZJ))
XSLOTS = 4
FAR = 1 << 20
BANK = 512
MAGIC = 0x5F3759DF
EPS = 1e-5

F32 = mybir.dt.float32
I32 = mybir.dt.int32
ALU = mybir.AluOpType
ACT = mybir.ActivationFunctionType

assert E % EJ == 0 and EGROUPS == NGROUPS


def sweep(eng, start, stop, front, back, step, slots=2):
    first, last = start + front, stop - back
    last -= (last - first) % slots
    for i in range(start, first):
        step(i, i % slots, False)
    with eng.Fori(first, last - slots + 1, slots) as i:
        for n in range(slots):
            step(i + n if n else i, (first + n) % slots, True)
    for i in range(last, stop):
        step(i, i % slots, False)


def per_slot(i, slot):
    return i * 8 + (16 - 8 * slot)


def per_slot4(i, slot):
    return i * 4 + (16 - 4 * slot)


def build(nc, x, src, dst, ea32, ea96, mW1, mb1, mW2, mb2, gW1, gb1, gW2, gb2, uW1, ub1, uW2, ub2,
          ln_g, ln_b, Wq, bq, Wk, bk, We, be, Wv, bv, ident_c, heads_c, spare_c, bounds_c, out):
    with ExitStack() as ctx:
        def sb(name, shape, dt=F32):
            return ctx.enter_context(nc.sbuf_tensor(name, shape, dt))

        def sem(name):
            return ctx.enter_context(nc.semaphore(name))

        agg_d = nc.dram_tensor("agg_d", [ZSTEPS * P * ZJ, D], F32).ap()
        x1_d = agg_d[0:N, :]
        cont_d = nc.dram_tensor("cont_d", [1, EGROUPS * EROWS + EJ], F32).ap()

        ident = sb("ident", [P, P])
        heads = sb("heads", [D, DH])
        mW1s, gW1s = sb("mW1s", [P, D]), sb("gW1s", [P, D])
        mW2s, gW2c, gW2s = sb("mW2s", [D, D]), sb("gW2c", [D, 1]), sb("gW2s", [D, D])
        uW1x, uW1a, uW2s = sb("uW1x", [D, D]), sb("uW1a", [D, D]), sb("uW2s", [D + 1, D])
        centre = sb("centre", [D, D])
        uW2m = sb("uW2m", [D + 1, 2])
        Wqs, Wks, Wes, Wvs = sb("Wqs", [D, D]), sb("Wks", [D, D]), sb("Wes", [D, D]), sb("Wvs", [D, DH])
        mb1s, gb1s, mb2s, gb2s, ub1s = (sb(n, [D, 1]) for n in ("mb1s", "gb1s", "mb2s", "gb2s", "ub1s"))
        bqs, bks, bes, bvs = sb("bqs", [D, 1]), sb("bks", [D, 1]), sb("bes", [D, 1]), sb("bvs", [DH, 1])
        lng, lnb = sb("lng", [P, D]), sb("lnb", [P, D])
        zeros = sb("zeros", [P, ZJ * D])
        src_i, dst_i, next_i = (sb(n, [P, EGROUPS, EJ], I32) for n in ("src_i", "dst_i", "next_i"))
        spare = sb("spare", [P, EGROUPS, EJ], I32)
        group_dst = sb("group_dst", [1, EGROUPS + 1], I32)
        bounds = sb("bounds", [1, 2, NGROUPS], I32)
        counts = sb("counts", [1, 2, EGROUPS])
        pairs = sb("pairs", [1, 2, 2, EGROUPS], I32)
        need = sb("need", [1, 2, 2, EGROUPS], I32)
        need_agg, need_x1 = need[:, :, 0, :], need[:, :, 1, :]
        same = sb("same", [P, EGROUPS, EJ])
        shift = sb("shift", [P, EGROUPS, EJ])
        add_at = sb("add_at", [P, EGROUPS, EJ], I32)
        put_at = sb("put_at", [P, EGROUPS, EJ], I32)
        dst_at = sb("dst_at", [P, EGROUPS, EJ], I32)
        rows = sb("rows", [P, EGROUPS * EJ, D])
        BELOW_GROUPS = -(-EGROUPS * NGROUPS // (EJ * D))
        below = (rows[0:1, (EGROUPS - BELOW_GROUPS) * EJ:, :].rearrange("a r f -> a (r f)")[:, 0:EGROUPS * NGROUPS]
                 .rearrange("a (e n) -> a e n", e=EGROUPS))

        x_in = sb("x_in", [P, XSLOTS, NJ * D])
        agg_in = sb("agg_in", [P, 2, NJ * D])
        nT = sb("nT", [D + 1, 2, NJ * P])
        hg, xb, y = (sb(n, [P, 2, NJ * D]) for n in ("hg", "xb", "y"))
        x1o, oo = sb("x1o", [P, 2, NJ * D]), sb("oo", [P, 2, NJ * D])
        bn = sb("bn", [P, 2, NJ, 6])
        mean, mdif, sqs, nv = (sb(n, [P, k, NJ]) for n, k in (("mean", 1), ("mdif", 2), ("sqs", 2), ("nv", 3)))
        nvar, nroot, nhalf = sb("nvar", [P, 3, NJ]), sb("nroot", [P, 3, NJ]), sb("nhalf", [P, 3, NJ])
        nscale, nshift = sb("nscale", [P, 2, 3, NJ]), sb("nshift", [P, 2, NJ])

        ein = sb("ein", [P, XSLOTS, EJ, D + DE])
        einT = sb("einT", [P, 2, EROWS])
        xT = einT[0:D, :, :]
        hidden = [sb(n, [DH, EROWS]) for n in ("hidden0", "hidden1", "hidden2", "hidden3")]
        gm, gg, gate, mm = (t[0:D, :] for t in hidden)
        mask = sb("mask", [DH, 2, EROWS])
        seg = sb("seg", [DH, 2, EROWS])

        x1s, fin = (x_in[:, :, k * EJ * D:(k + 1) * EJ * D].rearrange("p s (j f) -> p s j f", j=EJ) for k in range(2))
        x1d = sb("x1d", [P, 2, EJ, D])
        ea = sb("ea", [P, 2, EJ, D])
        kS, kq, kqe = (t[0:D, :] for t in hidden[0:3])
        clip = hidden[3]
        score, msg = (sb(n, [DH, EROWS]) for n in ("score", "msg"))
        yc = sb("yc", [P, 2, EJ, D])
        hc = sb("hc", [P, EJ, D])
        zr = sb("zr", [P, 2, EJ, HEADS])
        cbn = sb("cbn", [P, EJ, 6])
        csum, cdif, csqs, cv = (sb(n, [P, EJ]) for n in ("csum", "cdif", "csqs", "cv"))
        cvar, croot, chalf = sb("cvar", [P, EJ]), sb("croot", [P, EJ]), sb("chalf", [P, EJ])
        cscale, cshift = sb("cscale", [P, 2, EJ]), sb("cshift", [P, 2, EJ])

        ps = ctx.enter_context(nc.psum_tensor("ps", [P, 8, BANK], F32))

        def two_banks(b):
            return ps[:, b:b + 2, 0:EJ * D]

        nTf = nT[0:D, :, :].rearrange("p s c -> p (s c)")
        opT = [[nTf[:, 0:512], nTf[:, 512:1024], nTf[:, 1024:1536]],
               [nTf[:, 1536:2048], einT[0:D, 0, :], einT[0:D, 1, :]]]

        pads_set = sem("pads_set")
        edge_weights_loaded = sem("edge_weights_loaded")
        weights_loaded, src_loaded, index_loaded = sem("weights_loaded"), sem("src_loaded"), sem("index_loaded")
        centre_step = sem("centre_step")
        index_made, same_made, cont_stored = sem("index_made"), sem("same_made"), sem("cont_stored")
        needs_step, needs_made = sem("needs_step"), sem("needs_made")
        weights_made, zeros_stored = sem("weights_made"), sem("zeros_stored")
        xs_gathered = [[sem(f"xs_gathered{t}_{j}") for j in range(EJ)] for t in range(2)]
        ein_loaded = [sem(f"ein_loaded{s}") for s in range(XSLOTS)]
        ein_turned, einT_copied = sem("ein_turned"), sem("einT_copied")
        hidden_summed, gelu_done = sem("hidden_summed"), sem("gelu_done")
        message_summed, gate_summed = sem("message_summed"), sem("gate_summed")
        tanh_done, gate_done, gated = sem("tanh_done"), sem("gate_done"), sem("gated")
        mask_loaded = [sem("mask_loaded0"), sem("mask_loaded1")]
        scanned, agg_summed, agg_copied = sem("scanned"), sem("agg_summed"), sem("agg_copied")
        agg_added = [[sem(f"agg_added{t}_{j}") for j in range(EJ)] for t in range(2)]
        agg_loaded = [sem("agg_loaded0"), sem("agg_loaded1")]
        x_loaded = [sem(f"x_loaded{s}") for s in range(XSLOTS)]
        x_turned, xT_copied, node_summed = sem("x_turned"), sem("xT_copied"), sem("node_summed")
        x_centred = sem("x_centred")
        node_gelu, update_summed = sem("node_gelu"), sem("update_summed")
        hg_made, xb_made, w_made, y_made = sem("hg_made"), sem("xb_made"), sem("w_made"), sem("y_made")
        stats_step, root_step, norms_ready = sem("stats_step"), sem("root_step"), sem("norms_ready")
        h_measured, y_measured = sem("h_measured"), sem("y_measured")
        x1_made, out_made = sem("x1_made"), sem("out_made")
        x1_stored = [sem("x1_stored0"), sem("x1_stored1")]
        out_stored = [sem("out_stored0"), sem("out_stored1")]
        xd_gathered = [[sem(f"xd_gathered{t}_{j}") for j in range(EJ)] for t in range(2)]
        x1s_gathered = [[sem(f"x1s_gathered{t}_{j}") for j in range(EJ)] for t in range(2)]
        x1d_loaded = [sem("x1d_loaded0"), sem("x1d_loaded1")]
        ea_loaded = [sem("ea_loaded0"), sem("ea_loaded1")]
        cmask_loaded = [sem("cmask_loaded0"), sem("cmask_loaded1")]
        ops_turned, opsT_copied = sem("ops_turned"), sem("opsT_copied")
        k_summed, q_summed, e_summed, v_summed = (sem(n) for n in ("k_summed", "q_summed", "e_summed", "v_summed"))
        k_biased, kq_made, kqe_made = sem("k_biased"), sem("kq_made"), sem("kqe_made")
        heads_summed, clipped, score_made = sem("heads_summed"), sem("clipped"), sem("score_made")
        weighed, cscanned, seg_turned = sem("weighed"), sem("cscanned"), sem("seg_turned")
        z_step, hc_made, yc_made = sem("z_step"), sem("hc_made"), sem("yc_made")
        cstats_step, croot_step, cnorm_ready = sem("cstats_step"), sem("croot_step"), sem("cnorm_ready")
        fin_made = sem("fin_made")
        out_scattered = [[sem(f"out_scattered{t}_{j}") for j in range(EJ)] for t in range(2)]

        edge_weights = [(ident, ident_c), (mW1s, mW1), (gW1s, gW1), (mW2s, mW2), (gW2c, gW2), (uW1a, uW1[D:2 * D, :])]
        edge_biases = [(mb1s, mb1), (gb1s, gb1), (mb2s, mb2)]
        weights = [(heads, heads_c), (uW1x, uW1[0:D, :]), (Wqs, Wq), (Wks, Wk), (Wes, We)]
        biases = [(ub1s, ub1), (bqs, bq), (bks, bk), (bes, be)]
        EDGE_WEIGHTS = 16 * (len(edge_weights) + len(edge_biases) + 1)
        WEIGHTS = 16 * (len(weights) + len(biases) + 6)

        def slot_total(slot):
            return 16 * len(range(slot, NGROUPS, 2))

        def node_rows(t, g):
            at = min(g * NROWS, N - NROWS) if isinstance(g, int) else g * NROWS
            return t[bass.DynSlice(at, NROWS), :].rearrange("(p j) f -> p (j f)", j=NJ)

        block = ctx.enter_context(nc.Block())

        @block.sync
        def _(sp):
            sp.wait_ge(pads_set, 6)
            sp.dma_start(src_i[:, 0:EFULL, :], src[0:EFULL * EROWS].rearrange("(g p j) -> p g j", p=P, j=EJ)).then_inc(src_loaded, 16)
            sp.dma_start(src_i[0:ETAIL_P, EFULL, :], src[EFULL * EROWS:E].rearrange("(p j) -> p j", j=EJ)).then_inc(src_loaded, 16)
            sp.dma_start(spare[:], spare_c).then_inc(index_loaded, 16)
            sp.dma_start(dst_i[:, 0:EFULL, :], dst[0:EFULL * EROWS].rearrange("(g p j) -> p g j", p=P, j=EJ)).then_inc(index_loaded, 16)
            sp.dma_start(dst_i[0:ETAIL_P, EFULL, :], dst[EFULL * EROWS:E].rearrange("(p j) -> p j", j=EJ)).then_inc(index_loaded, 16)
            sp.dma_start(next_i[:, 0:EFULL, :], dst[1:EFULL * EROWS + 1].rearrange("(g p j) -> p g j", p=P, j=EJ)).then_inc(index_loaded, 16)
            sp.dma_start(next_i[0:ETAIL_P - 1, EFULL, :], dst[EFULL * EROWS + 1:E - EJ + 1].rearrange("(p j) -> p j", j=EJ)).then_inc(index_loaded, 16)
            sp.dma_start(bounds[:], bounds_c).then_inc(index_loaded, 16)
            sp.dma_start(next_i[ETAIL_P - 1:ETAIL_P, EFULL, 0:EJ - 1], dst[E - EJ + 1:E].rearrange("(a j) -> a j", a=1)).then_inc(index_loaded, 16)

            def edge_step(i, q, inner, zeroing=False):
                s, t = q % 2, (q + 2) % XSLOTS
                if inner or i + 2 < EGROUPS:
                    if inner or i >= 2:
                        sp.wait_ge(ein_turned, i - 1)
                    for j in range(EJ):
                        sp.wait_ge(xs_gathered[s][j], per_slot(i + 2, s))
                    sp.dma_start(ein[:, t, :, 0:D], rows[:, bass.DynSlice(i * EJ + 2 * EJ, EJ), :]).then_inc(ein_loaded[t], 16)
                    if isinstance(i, int) and i + 2 == EFULL:
                        sp.dma_start(ein[0:ETAIL_P, t, :, D:D + DE], ea32[EFULL * EROWS:E, :].rearrange("(p j) f -> p j f", j=EJ)).then_inc(ein_loaded[t], 16)
                    else:
                        sp.dma_start(ein[:, t, :, D:D + DE], ea32[bass.DynSlice(i * EROWS + 2 * EROWS, EROWS), :].rearrange("(p j) f -> p j f", j=EJ)).then_inc(ein_loaded[t], 16)
                if not inner and i == -2:
                    sp.wait_ge(same_made, 1)
                    sp.dma_start(cont_d[:, 0:1], zeros[0:1, 0:1]).then_inc(cont_stored, 16)
                    sp.dma_start(cont_d[:, 1:1 + EGROUPS * EROWS].rearrange("a (g p j) -> (a p) g j", p=P, j=EJ), same[:]).then_inc(cont_stored, 16)
                if inner or -1 <= i < EGROUPS - 1:
                    sp.wait_ge(cont_stored, 32)
                    if inner or i >= 1:
                        sp.wait_ge(scanned, i)
                    sp.dma_start(mask[0:D, 1 - s, :], cont_d[:, bass.DynSlice(i * EROWS + EROWS, EROWS)].broadcast_to([D, EROWS])).then_inc(mask_loaded[1 - s], 16)
                if zeroing:
                    sp.dma_start(agg_d[bass.DynSlice(i * P * ZJ + 2 * P * ZJ, P * ZJ), :].rearrange("(p j) f -> p (j f)", j=ZJ), zeros[:]).then_inc(zeros_stored, 16)

            sweep(sp, -2, ZSTEPS - 2, 4, 0, lambda i, q, inner: edge_step(i, q, inner, True), XSLOTS)
            sweep(sp, ZSTEPS - 2, EGROUPS - 1, 0, 2, edge_step, XSLOTS)

            sp.wait_ge(needs_made, 1)

            def update_step(i, q, inner):
                s = q % 2
                if inner or 0 <= i + 3 < NGROUPS:
                    if inner or i >= 1:
                        sp.wait_ge(xb_made, i)
                    sp.dma_start(x_in[:, (q + 3) % XSLOTS, :], node_rows(x, i + 3)).then_inc(x_loaded[(q + 3) % XSLOTS], 16)
                if inner or 0 <= i + 2 < NGROUPS:
                    if inner or i >= 0:
                        sp.wait_ge(node_summed, i + 1)
                    needs = [sp.value_load(need_agg[0:1, t, bass.DynSlice(i + 2, 1)], min_val=16, max_val=slot_total(0))
                             for t in range(2)]
                    for t in range(2):
                        for j in range(EJ):
                            sp.wait_ge(agg_added[t][j], needs[t])
                    sp.wait_ge(zeros_stored, 16 * ZSTEPS)
                    sp.dma_start(agg_in[:, s, :], node_rows(agg_d, i + 2)).then_inc(agg_loaded[s], 16)
                if inner or 5 <= i < NGROUPS + 5:
                    sp.wait_ge(x1_made, i - 4)
                    if isinstance(i, int) and i == NGROUPS + 4:
                        sp.wait_ge(x1_stored[s], slot_total(s))
                    sp.dma_start(node_rows(x1_d, i - 5), x1o[:, 1 - s, :]).then_inc(x1_stored[1 - s], 16)
                if inner or i >= 6:
                    sp.wait_ge(out_made, i - 5)
                    if isinstance(i, int) and i == NGROUPS + 5:
                        sp.wait_ge(out_stored[1 - s], slot_total(1 - s))
                    sp.dma_start(node_rows(out, i - 6), oo[:, s, :]).then_inc(out_stored[s], 16)

            sweep(sp, -3, NGROUPS + 6, 9, 10, update_step, XSLOTS)

            def attend_step(i, s, inner):
                if inner or i + 1 < EGROUPS:
                    if inner or i >= 1:
                        sp.wait_ge(ops_turned, i * 3)
                    for j in range(EJ):
                        sp.wait_ge(xd_gathered[1 - s][j], per_slot(i + 1, 1 - s))
                    sp.dma_start(x1d[:, 1 - s, :, :], rows[:, bass.DynSlice(i * EJ + EJ, EJ), :]).then_inc(x1d_loaded[1 - s], 16)
                    if isinstance(i, int) and i + 1 == EFULL:
                        sp.dma_start(ea[0:ETAIL_P, 1 - s, :, :], ea96[EFULL * EROWS:E, :].rearrange("(p j) f -> p j f", j=EJ)).then_inc(ea_loaded[1 - s], 16)
                    else:
                        sp.dma_start(ea[:, 1 - s, :, :], ea96[bass.DynSlice(i * EROWS + EROWS, EROWS), :].rearrange("(p j) f -> p j f", j=EJ)).then_inc(ea_loaded[1 - s], 16)
                if inner or i + 1 < EGROUPS:
                    sp.wait_ge(cont_stored, 32)
                    if inner or i >= 1:
                        sp.wait_ge(cscanned, i)
                    sp.dma_start(mask[:, 1 - s, :], cont_d[:, bass.DynSlice(i * EROWS + EROWS, EROWS)].broadcast_to([DH, EROWS])).then_inc(cmask_loaded[1 - s], 16)

            sweep(sp, -1, EGROUPS - 1, 3, 1, attend_step)
            for j in range(EJ):
                for t in range(2):
                    sp.wait_ge(out_scattered[t][j], slot_total(t))

        @block.gpsimd
        def _(pool):
            def rows_at(index, g, j):
                return bass.IndirectOffsetOnAxis(ap=index[:, g, j:j + 1], axis=0)

            pool.wait_ge(src_loaded, 32)
            for g in range(EGROUPS):
                if g == EGROUPS - BELOW_GROUPS:
                    pool.wait_ge(needs_step, 6)
                for j in range(EJ):
                    if g >= 2:
                        pool.wait_ge(xs_gathered[g % 2][j], per_slot(g - 2, g % 2))
                    pool.indirect_dma_start(rows[:, g * EJ + j, :], None, x, rows_at(src_i, g, j)).then_inc(xs_gathered[g % 2][j], 16)
            pool.wait_ge(index_made, 3)
            pool.wait_ge(zeros_stored, 16 * ZSTEPS)
            for g in range(EGROUPS):
                pool.wait_ge(agg_copied, g + 1)
                for j in range(EJ):
                    if g >= 2:
                        pool.wait_ge(agg_added[g % 2][j], per_slot(g - 2, g % 2))
                    pool.indirect_dma_start(agg_d, rows_at(add_at, g, j), rows[:, g * EJ + j, :], None,
                                            bounds_check=N + 2 * EROWS - 1, oob_is_err=True,
                                            compute_op=ALU.add).then_inc(agg_added[g % 2][j], 16)
            pool.wait_ge(needs_made, 1)
            for g in range(EGROUPS):
                needs = [pool.value_load(need_x1[0:1, s, g:g + 1], min_val=16, max_val=slot_total(0)) for s in range(2)]
                for j in range(EJ):
                    if g < 2:
                        pool.wait_ge(agg_added[g % 2][j], slot_total(g % 2))
                    else:
                        pool.wait_ge(xd_gathered[g % 2][j], per_slot(g - 2, g % 2))
                for s in range(2):
                    pool.wait_ge(x1_stored[s], needs[s])
                for j in range(EJ):
                    pool.indirect_dma_start(rows[:, g * EJ + j, :], None, x1_d, rows_at(dst_at, g, j)).then_inc(xd_gathered[g % 2][j], 16)
            for s in range(2):
                pool.wait_ge(x1_stored[s], slot_total(s))
            LAG = 8
            for g in range(EGROUPS + LAG):
                if g < EGROUPS:
                    if g >= XSLOTS:
                        pool.wait_ge(ops_turned, 3 * (g - XSLOTS + 1))
                    for j in range(EJ):
                        if g >= 2:
                            pool.wait_ge(x1s_gathered[g % 2][j], per_slot(g - 2, g % 2))
                        pool.indirect_dma_start(x1s[:, g % XSLOTS, j, :], None, x1_d, rows_at(src_i, g, j)).then_inc(x1s_gathered[g % 2][j], 16)
                b = g - LAG
                if b == 0:
                    for s in range(2):
                        pool.wait_ge(out_stored[s], slot_total(s))
                if b >= 0:
                    pool.wait_ge(fin_made, b + 1)
                    for j in range(EJ):
                        if b >= 2:
                            pool.wait_ge(out_scattered[b % 2][j], per_slot(b - 2, b % 2))
                        pool.indirect_dma_start(out, rows_at(put_at, b, j), fin[:, b % XSLOTS, j, :], None,
                                                bounds_check=N - 1, oob_is_err=False).then_inc(out_scattered[b % 2][j], 16)

        @block.tensor
        def _(pe):
            pe.wait_ge(edge_weights_loaded, EDGE_WEIGHTS)
            pe.wait_ge(weights_made, 3)

            def turn(to, of, last=None):
                mmx = pe.transpose(to, of, ident[:, :])
                if last is not None:
                    mmx.then_inc(last, 1)

            def edge_step(i, q, inner):
                s, t = q % 2, (q + 1) % XSLOTS
                if inner or 0 <= i < EGROUPS:
                    pe.wait_ge(einT_copied, i + 1)
                    if inner or i >= 1:
                        pe.wait_ge(gelu_done, i * 2)
                    pe.matmul(ps[0:D, 2, :], mW1s[:, :], einT[:, s, :], start=True, stop=True).then_inc(hidden_summed, 1)
                    pe.matmul(ps[0:D, 3, :], gW1s[:, :], einT[:, s, :], start=True, stop=True).then_inc(hidden_summed, 1)
                if inner or i + 1 < EGROUPS:
                    pe.wait_ge(ein_loaded[t], (i + 1) * 8 + (32 - 8 * t))
                    if inner or i >= 1:
                        pe.wait_ge(einT_copied, i)
                    to = ps[:, 1 - s, :].rearrange("p (c j) -> p j c", j=EJ)
                    for j in range(EJ):
                        turn(to[:, j, :], ein[:, t, j, :], ein_turned if j == EJ - 1 else None)
                if inner or 0 <= i < EGROUPS:
                    pe.wait_ge(gelu_done, i * 2 + 1)
                    if inner or i >= 1:
                        pe.wait_ge(gated, i)
                    pe.matmul(ps[0:D, 4, :], mW2s[:, :], gm[:, :], start=True, stop=True).then_inc(message_summed, 1)
                    pe.wait_ge(gelu_done, i * 2 + 2)
                    if inner or i >= 1:
                        pe.wait_ge(tanh_done, i)
                    pe.matmul(ps[0:D, 5, :], gW2s[:, :], gg[:, :], start=True, stop=True).then_inc(gate_summed, 1)
                if inner or i >= 1:
                    pe.wait_ge(scanned, i)
                    if inner or i >= 3:
                        pe.wait_ge(agg_copied, i - 2)
                    of = seg[0:D, 1 - s, :].rearrange("p (c j) -> p j c", j=EJ)
                    for j in range(EJ):
                        m = pe.matmul(ps[:, 6 + (1 - s), j * D:(j + 1) * D], of[:, j, :], uW1a[:, :], start=True, stop=True)
                    m.then_inc(agg_summed, 1)

            sweep(pe, -1, EGROUPS + 1, 4, 2, edge_step, XSLOTS)

            pe.wait_ge(weights_loaded, WEIGHTS)
            pe.wait_ge(weights_made, 7)
            pe.wait_ge(einT_copied, EGROUPS)
            pe.wait_ge(gelu_done, 2 * EGROUPS)
            pe.wait_ge(gated, EGROUPS)
            pe.wait_ge(tanh_done, EGROUPS)
            pe.wait_ge(agg_copied, EGROUPS)

            def update_step(i, q, inner):
                s = q % 2
                if inner or i + 1 < NGROUPS:
                    pe.wait_ge(x_loaded[(q + 1) % XSLOTS], per_slot4(i + 1, (q + 1) % XSLOTS))
                    if inner or i >= 0:
                        pe.wait_ge(xT_copied, i + 1)
                    for j in range(NJ):
                        turn(ps[0:D, j // 4, (j % 4) * P:(j % 4 + 1) * P], x_in[:, (q + 1) % XSLOTS, j * D:(j + 1) * D],
                             x_turned if j == NJ - 1 else None)
                if inner or i >= 0:
                    pe.wait_ge(node_gelu, i + 1)
                    for j in range(NJ):
                        m = pe.matmul(ps[:, 4 + 2 * s + j // 4, (j % 4) * D:(j % 4 + 1) * D],
                                      nT[:, s, j * P:(j + 1) * P], uW2s[:, :], start=False, stop=j % 4 == 3)
                    m.then_inc(update_summed, 1)
                if inner or i + 1 < NGROUPS:
                    pe.wait_ge(xT_copied, i + 2)
                    if inner or i >= 0:
                        pe.wait_ge(node_gelu, i + 1)
                    for b in range(2):
                        pe.matmul(ps[0:D, 2 + b, :], uW1x[:, :], xT[:, b, :], start=True, stop=False)
                    pe.wait_ge(agg_loaded[1 - s], per_slot(i + 1, 1 - s))
                    for j in range(NJ):
                        m = pe.matmul(ps[0:D, 2 + j // 4, (j % 4) * P:(j % 4 + 1) * P],
                                      agg_in[:, 1 - s, j * D:(j + 1) * D], ident[:, :], start=False, stop=j % 4 == 3)
                    m.then_inc(node_summed, 1)
                    if inner or i >= 1:
                        pe.wait_ge(hg_made, i)
                    for j in range(NJ):
                        m = pe.matmul(ps[:, 4 + 2 * (1 - s) + j // 4, (j % 4) * D:(j % 4 + 1) * D],
                                      xT[:, j // 4, (j % 4) * P:(j % 4 + 1) * P], centre[:, :], start=j % 4 == 0, stop=False)
                    m.then_inc(x_centred, 1)

            sweep(pe, -1, NGROUPS, 3, 1, update_step, XSLOTS)

            pe.wait_ge(node_gelu, NGROUPS)
            pe.wait_ge(hg_made, NGROUPS)

            def attend_step(i, q, inner):
                s = q % 2
                if inner or 0 <= i < EGROUPS:
                    pe.wait_ge(opsT_copied, i * 3 + 3)
                    xsT, xdT, eaT = opT[s]
                    if inner or i >= 1:
                        pe.wait_ge(k_biased, i)
                    pe.matmul(ps[0:D, 3, :], Wks[:, :], xsT, start=True, stop=True).then_inc(k_summed, 1)
                    if inner or i >= 1:
                        pe.wait_ge(kq_made, i)
                    pe.matmul(ps[0:D, 4, :], Wqs[:, :], xdT, start=True, stop=True).then_inc(q_summed, 1)
                    if inner or i >= 1:
                        pe.wait_ge(clipped, i)
                    pe.matmul(ps[0:D, 5, :], Wes[:, :], eaT, start=True, stop=True).then_inc(e_summed, 1)
                    if inner or i >= 1:
                        pe.wait_ge(weighed, i)
                    pe.matmul(ps[0:DH, 6, :], Wvs[:, :], xsT, start=True, stop=True).then_inc(v_summed, 1)
                if inner or i >= 1:
                    pe.wait_ge(cscanned, i)
                    if inner or i >= 2:
                        pe.wait_ge(hc_made, i - 1)
                    of = seg[:, 1 - s, :].rearrange("p (c j) -> p j c", j=EJ)
                    for j in range(EJ):
                        m = pe.transpose(ps[:, 7, j * DH:(j + 1) * DH], of[:, j, :], ident[0:DH, 0:DH])
                    m.then_inc(seg_turned, 1)
                if inner or i + 1 < EGROUPS:
                    for j in range(EJ):
                        pe.wait_ge(x1s_gathered[1 - s][j], per_slot(i + 1, 1 - s))
                    pe.wait_ge(x1d_loaded[1 - s], per_slot(i + 1, 1 - s))
                    pe.wait_ge(ea_loaded[1 - s], per_slot(i + 1, 1 - s))
                    if inner or i >= 0:
                        pe.wait_ge(opsT_copied, i * 3 + 3)
                    for b, (of, t) in enumerate(((x1s, (q + 1) % XSLOTS), (x1d, 1 - s), (ea, 1 - s))):
                        to = ps[0:D, b, :].rearrange("p (c j) -> p j c", j=EJ)
                        for j in range(EJ):
                            turn(to[:, j, :], of[:, t, j, :], ops_turned if j == EJ - 1 else None)
                if inner or 0 <= i < EGROUPS:
                    pe.wait_ge(kqe_made, i + 1)
                    pe.matmul(ps[0:DH, 5, :], heads[:, :], kqe[:, :], start=True, stop=True).then_inc(heads_summed, 1)

            sweep(pe, -1, EGROUPS + 1, 4, 2, attend_step, XSLOTS)

        @block.scalar
        def _(act):
            column = lambda t: t.rearrange("(d a) -> d a", a=1)
            row = lambda t: t.rearrange("(a d) -> a d", a=1)
            for to, of in edge_weights:
                act.dma_start(to[:], of).then_inc(edge_weights_loaded, 16)
            for to, of in edge_biases:
                act.dma_start(to[:], column(of)).then_inc(edge_weights_loaded, 16)
            act.dma_start(gb2s[:], column(gb2).broadcast_to([D, 1])).then_inc(edge_weights_loaded, 16)
            for to, of in weights:
                act.dma_start(to[:], of).then_inc(weights_loaded, 16)
            for to, of in biases:
                act.dma_start(to[:], column(of)).then_inc(weights_loaded, 16)
            act.dma_start(uW2s[0:D, :], uW2).then_inc(weights_loaded, 16)
            act.dma_start(uW2s[D:D + 1, :], row(ub2)).then_inc(weights_loaded, 16)
            for to, of in ((lng, ln_g), (lnb, ln_b)):
                act.dma_start(to[:], row(of).broadcast_to([P, D])).then_inc(weights_loaded, 16)
            act.wait_ge(pads_set, 6)
            act.dma_start(Wvs[:, 0:D], Wv).then_inc(weights_loaded, 16)
            act.dma_start(bvs[0:D, :], column(bv)).then_inc(weights_loaded, 16)
            act.wait_ge(edge_weights_loaded, EDGE_WEIGHTS)
            act.wait_ge(weights_made, 5)

            def edge_step(i, s, inner):
                if inner or i >= 0:
                    act.wait_ge(hidden_summed, i * 2 + 1)
                    if inner or i >= 1:
                        act.wait_ge(message_summed, i)
                    act.activation(gm[:, :], ps[0:D, 2, :], ACT.Gelu, bias=mb1s[:, 0:1]).then_inc(gelu_done, 1)
                    act.wait_ge(hidden_summed, i * 2 + 2)
                    if inner or i >= 1:
                        act.wait_ge(gate_summed, i)
                    act.activation(gg[:, :], ps[0:D, 3, :], ACT.Gelu, bias=gb1s[:, 0:1]).then_inc(gelu_done, 1)
                if inner or i + 1 < EGROUPS:
                    act.wait_ge(ein_turned, i + 2)
                    if inner or i >= 1:
                        act.wait_ge(hidden_summed, i * 2)
                    act.activation(einT[:, 1 - s, :], ps[:, 1 - s, :], ACT.Copy).then_inc(einT_copied, 1)
                if inner or i >= 0:
                    act.wait_ge(gate_summed, i + 1)
                    if inner or i >= 1:
                        act.wait_ge(gated, i)
                    act.activation(gate[:, :], ps[0:D, 5, :], ACT.Tanh, bias=gb2s[:, 0:1], scale=0.5).then_inc(tanh_done, 1)

            sweep(act, -1, EGROUPS, 4, 1, edge_step)
            act.wait_ge(weights_loaded, WEIGHTS)

            def update_step(i, s, inner):
                k = 1 - s
                if inner or i + 1 < NGROUPS:
                    act.wait_ge(x_turned, i + 2)
                    if inner or i >= 0:
                        act.wait_ge(x_centred, i + 1)
                    act.activation(xT, ps[0:D, 0:2, :], ACT.Copy).then_inc(xT_copied, 1)
                if inner or i >= 4:
                    act.wait_ge(norms_ready, i * 2)
                if inner or 4 <= i < NGROUPS + 4:
                    if inner or i >= 6:
                        act.wait_ge(x1_stored[s], per_slot(i - 6, s))
                        act.wait_ge(out_made, i - 5)
                    for j in range(NJ):
                        o = act.activation(x1o[:, s, j * D:(j + 1) * D], y[:, s, j * D:(j + 1) * D], ACT.Identity,
                                           bias=nshift[:, k, j:j + 1], scale=nscale[:, k, 1, j:j + 1])
                    o.then_inc(x1_made, 1)
                def output(a, b):
                    if inner or i >= 5:
                        for j in range(a, b):
                            o = act.activation(oo[:, 1 - s, j * D:(j + 1) * D], x1o[:, 1 - s, j * D:(j + 1) * D], ACT.Identity,
                                               scale=nscale[:, k, 2, j:j + 1])
                        if b == NJ:
                            o.then_inc(out_made, 1)

                if inner or i >= 5:
                    if inner or i >= 7:
                        act.wait_ge(out_stored[1 - s], per_slot(i - 7, 1 - s))
                    act.wait_ge(x1_made, i - 4)
                output(0, NJ // 2)
                if inner or i + 1 < NGROUPS:
                    act.wait_ge(node_summed, i + 2)
                    if inner or i >= 1:
                        act.wait_ge(update_summed, i)
                    act.activation(nT[0:D, 1 - s, :].rearrange("p (b c) -> p b c", b=2), ps[0:D, 2:4, :], ACT.Gelu, bias=ub1s[:, 0:1]).then_inc(node_gelu, 1)
                output(NJ // 2, NJ)

            sweep(act, -1, NGROUPS + 5, 8, 6, update_step)

            def attend_step(i, q, inner):
                s = q % 2
                if inner or 0 <= i < EGROUPS:
                    act.wait_ge(k_summed, i + 1)
                    if inner or i >= 1:
                        act.wait_ge(kq_made, i)
                    act.activation(kS[:, :], ps[0:D, 3, :], ACT.Identity, bias=bks[:, 0:1]).then_inc(k_biased, 1)
                if inner or i >= 3:
                    act.wait_ge(cnorm_ready, i - 2)
                    if inner or i >= 7:
                        for j in range(EJ):
                            act.wait_ge(out_scattered[1 - s][j], per_slot(i - 7, 1 - s))
                    for j in range(EJ):
                        o = act.activation(fin[:, (q + 1) % XSLOTS, j, :], yc[:, 1 - s, j, :], ACT.Identity,
                                           bias=cshift[:, 1 - s, j:j + 1], scale=cscale[:, 1 - s, j:j + 1])
                    o.then_inc(fin_made, 1)
                if inner or i + 1 < EGROUPS:
                    for b in range(3):
                        act.wait_ge(ops_turned, i * 3 + 4 + b)
                        if b == 0 and (inner or i >= 1):
                            act.wait_ge(v_summed, i)
                            act.wait_ge(e_summed, i)
                            act.wait_ge(q_summed, i)
                        act.activation(opT[1 - s][b], ps[0:D, b, :], ACT.Copy).then_inc(opsT_copied, 1)
                if inner or 0 <= i < EGROUPS:
                    act.wait_ge(clipped, i + 1)
                    if inner or i >= 1:
                        act.wait_ge(weighed, i)
                    act.activation(score[:, :], clip[:, :], ACT.Exp).then_inc(score_made, 1)

            sweep(act, -1, EGROUPS + 3, 8, 4, attend_step, XSLOTS)

        @block.vector
        def _(dve):
            dve.memset(src_i[:, EFULL, :], 0).then_inc(pads_set, 1)
            dve.memset(dst_i[:, EFULL, :], FAR).then_inc(pads_set, 1)
            dve.memset(next_i[:, EFULL, :], FAR).then_inc(pads_set, 1)
            dve.memset(zeros[:, :], 0.0).then_inc(pads_set, 1)
            dve.memset(Wvs[:, :], 0.0).then_inc(pads_set, 1)
            dve.memset(bvs[:, :], 1.0).then_inc(pads_set, 1)
            dve.memset(nT[D:D + 1, :, :], 1.0).then_inc(weights_made, 1)
            dve.wait_ge(index_loaded, 16 * 7)
            dve.tensor_tensor(same[:, :, :], dst_i[:, :, :], next_i[:, :, :], ALU.is_equal).then_inc(same_made, 1)
            dve.tensor_tensor(shift[:, :, :], spare[:, :, :], dst_i[:, :, :], ALU.subtract).then_inc(same_made, 1)
            dve.tensor_scalar(dst_at[:, :, :], dst_i[:, :, :], N - 1, None, ALU.min).then_inc(index_made, 1)
            dve.wait_ge(same_made, 2)
            dve.tensor_tensor(shift[:, :, :], shift[:, :, :], same[:, :, :], ALU.mult).then_inc(same_made, 1)
            dve.scalar_tensor_tensor(put_at[:, :, :], same[:, :, :], float(FAR), dst_i[:, :, :], ALU.mult, ALU.add).then_inc(index_made, 1)
            dve.wait_ge(same_made, 3)
            dve.tensor_tensor(add_at[:, :, :], dst_i[:, :, :], shift[:, :, :], ALU.add).then_inc(index_made, 1)
            dve.wait_ge(pads_set, 6)
            dve.wait_ge(edge_weights_loaded, EDGE_WEIGHTS)
            dve.tensor_scalar(gW2s[:, :], zeros[0:D, 0:D], gW2c[:, 0:1], None, ALU.add).then_inc(weights_made, 1)
            dve.tensor_scalar(mW2s[:, :], mW2s[:, :], 0.5, None, ALU.mult).then_inc(weights_made, 1)
            dve.tensor_scalar(mb2s[:, :], mb2s[:, :], 0.5, None, ALU.mult).then_inc(weights_made, 1)
            dve.tensor_scalar(gb2s[:, :], gb2s[:, :], 0.5, None, ALU.mult).then_inc(weights_made, 1)

            wide = [1, EGROUPS, NGROUPS]

            def centre_update():
                dve.wait_ge(weights_loaded, WEIGHTS)
                dve.tensor_scalar(centre[:, :], ident[0:D, 0:D], -1.0 / D, None, ALU.add).then_inc(weights_made, 1)
                dve.tensor_reduce(uW2m[:, 0:1], uW2s[:, :], mybir.AxisListType.X, ALU.add).then_inc(centre_step, 1)
                dve.wait_ge(centre_step, 1)
                dve.tensor_scalar(uW2m[:, 1:2], uW2m[:, 0:1], 1.0 / D, None, ALU.mult).then_inc(centre_step, 1)
                dve.wait_ge(centre_step, 2)
                dve.tensor_scalar(uW2s[:, :], uW2s[:, :], uW2m[:, 1:2], None, ALU.subtract).then_inc(weights_made, 1)

            def needs(part):
                if part == 0:
                    dve.memset(group_dst[:, EGROUPS:], FAR).then_inc(needs_step, 1)
                    dve.tensor_copy(group_dst[:, 0:EGROUPS], dst_i[0:1, :, 0]).then_inc(needs_step, 1)
                    dve.wait_ge(needs_step, 2)
                    dve.tensor_tensor(below[:, :, :], group_dst[:, 0:EGROUPS].unsqueeze(1).broadcast_to(wide),
                                      bounds[:, 0, :].unsqueeze(2).broadcast_to(wide), ALU.is_lt).then_inc(needs_step, 1)
                if part == 2:
                    dve.wait_ge(needs_step, 4)
                    dve.tensor_tensor(below[:, :, :], bounds[:, 1, :].unsqueeze(1).broadcast_to(wide),
                                      group_dst[:, 1:].unsqueeze(2).broadcast_to(wide), ALU.is_le).then_inc(needs_step, 1)
                if part in (1, 3):
                    dve.wait_ge(needs_step, 2 + part)
                    dve.tensor_reduce(counts[:, part // 2, :], below[:, :, :], mybir.AxisListType.X, ALU.add).then_inc(needs_step, 1)
                if part == 3:
                    dve.wait_ge(needs_step, 6)
                    dve.tensor_scalar(pairs[:, 0, :, :], counts[:, :, :], 2.0, 1.0, ALU.max, ALU.add).then_inc(needs_step, 1)
                    dve.tensor_scalar(pairs[:, 1, :, :], counts[:, :, :], 2.0, None, ALU.max).then_inc(needs_step, 1)
                    dve.wait_ge(needs_step, 8)
                    dve.tensor_scalar(pairs[:], pairs[:], 1, None, ALU.arith_shift_right).then_inc(needs_step, 1)
                    dve.wait_ge(needs_step, 9)
                    dve.tensor_scalar(need[:], pairs[:], 16, None, ALU.mult).then_inc(needs_made, 1)


            dve.wait_ge(weights_made, 5)

            def edge_step(i, s, inner):
                if inner or i < EGROUPS:
                    dve.wait_ge(tanh_done, i + 1)
                    dve.tensor_scalar(gate[:, :], gate[:, :], 1.0, None, ALU.add).then_inc(gate_done, 1)
                    dve.wait_ge(gate_done, i + 1)
                    dve.wait_ge(message_summed, i + 1)
                    dve.scalar_tensor_tensor(mm[:, :], ps[0:D, 4, :], mb2s[:, 0:1], gate[:, :], ALU.add, ALU.mult).then_inc(gated, 1)
                    dve.wait_ge(gated, i + 1)
                    dve.wait_ge(mask_loaded[s], per_slot(i, s))
                    if inner or i >= 2:
                        dve.wait_ge(agg_summed, i - 1)
                    if inner or i >= 1:
                        dve.wait_ge(scanned, i)
                    before = seg[0:D, 1 - s, EROWS - 1:EROWS] if inner or i >= 1 else 0.0
                    dve.tensor_tensor_scan(seg[0:D, s, :], mask[0:D, s, :], mm[:, :], before, ALU.mult, ALU.add).then_inc(scanned, 1)
                if inner or i >= 1:
                    dve.wait_ge(agg_summed, i)
                    dve.tensor_copy(rows[:, bass.DynSlice(i * EJ - EJ, EJ), :],
                                    ps[:, 6 + (1 - s), 0:EJ * D].rearrange("p (j f) -> p j f", j=EJ)).then_inc(agg_copied, 1)
                if not inner and i < 4:
                    needs(i)
                if not inner and i == 3:
                    centre_update()

            sweep(dve, 0, EGROUPS + 1, 4, 1, edge_step)

            lng4 = lng[:, :].unsqueeze(1).unsqueeze(1).broadcast_to([P, 2, NJ // 2, D])
            lnbb = lnb[:, :].unsqueeze(1).broadcast_to([P, NJ, D])

            def rows_of(t, s):
                return t[:, s, :].rearrange("p (j f) -> p j f", j=NJ)

            def norm_op(k, apart, squares, var, with_eps, guess, half, done, base):
                gi, vi = guess.bitcast(I32), with_eps.bitcast(I32)
                dve.wait_ge(done, base + k)
                if k == 0:
                    ins = dve.scalar_tensor_tensor(apart, apart, 0.25, apart, ALU.mult, ALU.mult)
                elif k == 1:
                    ins = dve.scalar_tensor_tensor(var[0], squares, 1.0 / D, apart, ALU.mult, ALU.add)
                elif k == 2:
                    ins = dve.tensor_scalar(with_eps, var[1], EPS, None, ALU.add)
                elif k == 3:
                    ins = dve.tensor_scalar(gi, vi, 1, None, ALU.arith_shift_right)
                elif k == 4:
                    ins = dve.tensor_scalar(gi, gi, -1, MAGIC, ALU.mult, ALU.add)
                elif k % 3 == 2:
                    ins = dve.scalar_tensor_tensor(half, guess, -0.5, guess, ALU.mult, ALU.mult)
                elif k % 3 == 0:
                    ins = dve.tensor_tensor(half, half, with_eps, ALU.mult)
                else:
                    ins = dve.scalar_tensor_tensor(guess, half, 1.5, guess, ALU.add, ALU.mult)
                ins.then_inc(done, 1)

            for t, value in ((bn, 1.0), (nv, 1.0), (mdif, 0.0), (sqs, 1.0), (mean, 0.0)):
                dve.memset(t[:], value).then_inc(stats_step, 1)
            dve.wait_ge(stats_step, 5)
            NORM_OPS = 14
            NSTEPS = NORM_OPS + 5

            def root_base(i):
                return i * NSTEPS + 1

            dve.memset(nroot[:, :, :], 1.0).then_inc(root_step, 1)

            def update_step(i, q, inner):
                s = q % 2

                def norm(k):
                    norm_op(k, mdif[:, :, :], sqs[:, :, :], (nv[:, 0:2, :], nv[:, :, :]), nvar[:, :, :],
                            nroot[:, :, :], nhalf[:, :, :], root_step, root_base(i))

                if inner or i < NGROUPS:
                    dve.wait_ge(update_summed, i + 1)
                    if inner or i >= 1:
                        dve.wait_ge(root_step, root_base(i) - 1)
                    for j in range(NJ):
                        at = (j % 4) * D
                        b = dve.bn_stats(bn[:, 0, j, :], ps[:, 4 + 2 * s + j // 4, at:at + D])
                        if j == NJ - 1:
                            b.then_inc(h_measured, 1)
                        norm(j)
                else:
                    for k in range(NJ):
                        norm(k)
                with_y = inner or 2 <= i < NGROUPS + 2
                halves = lambda t: t[:, s, :].rearrange("p (b j f) -> p b j f", b=2, f=D)
                if with_y:
                    dve.wait_ge(norms_ready, i * 2)
                    if inner or i >= 4:
                        dve.wait_ge(x1_made, i - 3)
                    dve.wait_ge(hg_made, i - 1)
                    dve.tensor_tensor(rows_of(y, s), rows_of(hg, s), nscale[:, 1 - s, 0, :].unsqueeze(2).broadcast_to([P, NJ, D]), ALU.mult).then_inc(w_made, 1)
                norm(NJ)
                if inner or i < NGROUPS:
                    if with_y:
                        dve.wait_ge(w_made, i - 1)
                    dve.tensor_tensor(halves(hg), two_banks(4 + 2 * s).rearrange("p b (j f) -> p b j f", f=D), lng4, ALU.mult).then_inc(hg_made, 1)
                norm(NJ + 1)
                if with_y:
                    dve.wait_ge(w_made, i - 1)
                    dve.wait_ge(xb_made, i - 1)
                    dve.tensor_tensor(y[:, s, :], y[:, s, :], xb[:, s, :], ALU.add).then_inc(y_made, 1)
                norm(NJ + 2)

                done = root_base(i) + NORM_OPS

                def scales(k):
                    if k == 0:
                        if inner or i >= 5:
                            dve.wait_ge(x1_made, i - 4)
                        if inner or i >= 6:
                            dve.wait_ge(out_made, i - 5)
                        dve.wait_ge(root_step, done)
                        dve.tensor_copy(nscale[:, s, :, :], nroot[:, :, :]).then_inc(norms_ready, 1)
                    elif k == 1:
                        dve.scalar_tensor_tensor(nshift[:, s, :], mean[:, 0, :], -1.0, nroot[:, 1, :], ALU.mult, ALU.mult).then_inc(norms_ready, 1)
                        dve.tensor_tensor(nv[:, 2, :], nv[:, 1, :], nroot[:, 1, :], ALU.mult).then_inc(root_step, 1)
                    else:
                        dve.wait_ge(root_step, done + 1)
                        dve.tensor_tensor(nv[:, 2, :], nv[:, 2, :], nroot[:, 1, :], ALU.mult).then_inc(root_step, 1)

                if with_y:
                    dve.wait_ge(y_made, i - 1)
                for j in range(NJ):
                    if with_y:
                        b = dve.bn_stats(bn[:, 1, j, :], y[:, s, j * D:(j + 1) * D])
                        if j == NJ - 1:
                            b.then_inc(y_measured, 1)
                    if j < 3:
                        norm(NJ + 3 + j)
                    elif j < 6:
                        scales(j - 3)
                if inner or i < NGROUPS:
                    dve.tensor_tensor(rows_of(xb, s), x_in[:, q, :].rearrange("p (j f) -> p j f", j=NJ), lnbb, ALU.add).then_inc(xb_made, 1)
                if inner or i < NGROUPS:
                    dve.wait_ge(h_measured, i + 1)
                if with_y:
                    dve.wait_ge(y_measured, i - 1)
                dve.wait_ge(root_step, done + 2)
                dve.tensor_tensor(mdif[:, :, :], bn[:, :, :, 1], bn[:, :, :, 4], ALU.subtract).then_inc(root_step, 1)
                dve.tensor_tensor(sqs[:, :, :], bn[:, :, :, 2], bn[:, :, :, 5], ALU.add).then_inc(root_step, 1)
                dve.wait_ge(norms_ready, i * 2 + 2)
                dve.wait_ge(root_step, done + 3)
                dve.scalar_tensor_tensor(mean[:, 0, :], mdif[:, 1, :], -0.5, bn[:, 1, :, 1], ALU.mult, ALU.add).then_inc(root_step, 1)

            sweep(dve, 0, NGROUPS + 4, 7, 5, update_step, XSLOTS)

            def attend_step(i, s, inner):
                def norm(k):
                    if inner or 2 <= i < EGROUPS + 2:
                        norm_op(k, cdif[:, :], csqs[:, :], (cv[:, :], cv[:, :]), cvar[:, :], croot[:, :],
                                chalf[:, :], croot_step, i * 18 - 33)

                with_edges = inner or i < EGROUPS
                with_mean = inner or 1 <= i < EGROUPS + 1
                with_norm = inner or 2 <= i < EGROUPS + 2
                if with_edges:
                    dve.wait_ge(q_summed, i + 1)
                    dve.wait_ge(k_biased, i + 1)
                    dve.scalar_tensor_tensor(kq[:, :], ps[0:D, 4, :], bqs[:, 0:1], kS[:, :], ALU.add, ALU.mult).then_inc(kq_made, 1)
                if with_norm:
                    dve.wait_ge(cstats_step, i - 1)
                    if inner or i >= 3:
                        dve.wait_ge(cnorm_ready, i - 2)
                    dve.tensor_tensor(csum[:, :], cbn[:, :, 1], cbn[:, :, 4], ALU.add).then_inc(croot_step, 1)
                    dve.tensor_tensor(cdif[:, :], cbn[:, :, 1], cbn[:, :, 4], ALU.subtract).then_inc(croot_step, 1)
                    dve.tensor_tensor(csqs[:, :], cbn[:, :, 2], cbn[:, :, 5], ALU.add).then_inc(croot_step, 1)
                if with_edges:
                    dve.wait_ge(e_summed, i + 1)
                    dve.wait_ge(kq_made, i + 1)
                    if inner or i >= 1:
                        dve.wait_ge(heads_summed, i)
                    dve.scalar_tensor_tensor(kqe[:, :], ps[0:D, 5, :], bes[:, 0:1], kq[:, :], ALU.add, ALU.mult).then_inc(kqe_made, 1)
                norm(0)
                if with_mean:
                    dve.wait_ge(seg_turned, i)
                    back = ps[:, 7, 0:EJ * DH].rearrange("p (j f) -> p j f", j=EJ)
                    dve.tensor_scalar(zr[:, 0, :, :], back[:, :, D:DH], 1e-6, None, ALU.add).then_inc(z_step, 1)
                norm(1)
                if with_mean:
                    dve.wait_ge(z_step, i * 2 - 1)
                    dve.reciprocal(zr[:, 1, :, :], zr[:, 0, :, :]).then_inc(z_step, 1)
                norm(2)
                for j in range(EJ):
                    if with_mean:
                        dve.wait_ge(z_step, i * 2)
                        b = dve.tensor_tensor(hc[:, j, :].rearrange("p (a d) -> p a d", a=HEADS),
                                              back[:, j, 0:D].rearrange("p (a d) -> p a d", a=HEADS),
                                              zr[:, 1, j, :].unsqueeze(2).broadcast_to([P, HEADS, HD]), ALU.mult)
                        if j == EJ - 1:
                            b.then_inc(hc_made, 1)
                    norm(3 + j)
                if with_edges:
                    dve.wait_ge(heads_summed, i + 1)
                    if inner or i >= 1:
                        dve.wait_ge(score_made, i)
                    dve.tensor_scalar(clip[:, :], ps[0:DH, 5, :], -5.0, 5.0, ALU.max, ALU.min).then_inc(clipped, 1)
                norm(7)
                if with_mean:
                    dve.wait_ge(hc_made, i)
                    if inner or i >= 3:
                        dve.wait_ge(fin_made, i - 2)
                    dve.tensor_tensor(yc[:, 1 - s, :, :], hc[:, :, :], rows[:, bass.DynSlice(i * EJ - EJ, EJ), :], ALU.add).then_inc(yc_made, 1)
                norm(8)
                for j in range(EJ):
                    if with_mean:
                        dve.wait_ge(yc_made, i)
                        b = dve.bn_stats(cbn[:, j, :], yc[:, 1 - s, j, :])
                        if j == EJ - 1:
                            b.then_inc(cstats_step, 1)
                    norm(9 + j)
                if with_edges:
                    dve.wait_ge(score_made, i + 1)
                    dve.wait_ge(v_summed, i + 1)
                    dve.scalar_tensor_tensor(msg[:, :], ps[0:DH, 6, :], bvs[:, 0:1], score[:, :], ALU.add, ALU.mult).then_inc(weighed, 1)
                norm(13)
                if with_edges:
                    dve.wait_ge(weighed, i + 1)
                    dve.wait_ge(cmask_loaded[s], per_slot(i, s))
                    if inner or i >= 2:
                        dve.wait_ge(seg_turned, i - 1)
                    if inner or i >= 1:
                        dve.wait_ge(cscanned, i)
                    before = seg[:, 1 - s, EROWS - 1:EROWS] if inner or i >= 1 else 0.0
                    dve.tensor_tensor_scan(seg[:, s, :], mask[:, s, :], msg[:, :], before, ALU.mult, ALU.add).then_inc(cscanned, 1)
                if with_norm:
                    if inner or i >= 4:
                        dve.wait_ge(fin_made, i - 3)
                    dve.wait_ge(croot_step, i * 18 - 36 + 17)
                    dve.tensor_copy(cscale[:, s, :], croot[:, :]).then_inc(croot_step, 1)
                    dve.wait_ge(croot_step, i * 18 - 18)
                    dve.scalar_tensor_tensor(cshift[:, s, :], csum[:, :], -0.5, croot[:, :], ALU.mult, ALU.mult).then_inc(cnorm_ready, 1)

            sweep(dve, 0, EGROUPS + 2, 5, 3, attend_step)


_ORDER = ["x", "src", "dst", "edge_attr_32", "edge_attr_96"] + [
    f"L0_gnn_{n}" for n in ("mW1", "mb1", "mW2", "mb2", "gW1", "gb1", "gW2", "gb2", "uW1", "ub1", "uW2", "ub2", "ln_g", "ln_b")] + [
    f"L1_gnn_{n}" for n in ("Wq", "bq", "Wk", "bk", "We", "be", "Wv", "bv")]


def shape_constants():
    heads = np.zeros((D, DH), np.float32)
    for f in range(D):
        heads[f, f // HD * HD:(f // HD + 1) * HD] = HD ** -0.5
        heads[f, D + f // HD] = HD ** -0.5
    p, g, j = np.ogrid[0:P, 0:EGROUPS, 0:EJ]
    spare = (N + (g % 2) * EROWS + p + P * j).astype(np.int32)
    starts = np.minimum(np.arange(NGROUPS) * NROWS, N - NROWS)
    bounds = np.stack([starts + NROWS, starts])[None].astype(np.int32)
    return {"ident_c": np.eye(P, dtype=np.float32), "heads_c": heads, "spare_c": spare, "bounds_c": bounds}


def kernel(**inputs):
    import concourse.bacc as bacc
    from concourse.bass_utils import run_bass_kernel_spmd

    nc = bacc.Bacc("TRN2", target_bir_lowering=False, num_devices=1)
    arrays = {f"in_{n}": np.ascontiguousarray(inputs[n]) for n in _ORDER} | shape_constants()
    args = [nc.dram_tensor(n, a.shape, mybir.dt.from_np(a.dtype), kind="ExternalInput").ap() for n, a in arrays.items()]
    out = nc.dram_tensor("out", [N, D], F32, kind="ExternalOutput").ap()
    build(nc, *args, out)
    return run_bass_kernel_spmd(nc, [arrays], core_ids=[0]).results[0]["out"]
```
